# Optimizing a Trainium2 kernel written in Bass

```python
import numpy as np
import jax
import jax.numpy as jnp

def _softmax(x, axis=-1):
    return jax.nn.softmax(x, axis=axis)

def _gelu(x):
    return jax.nn.gelu(x, approximate=True)

def _silu(x):
    return jax.nn.silu(x)

def _sigmoid(x):
    return jax.nn.sigmoid(x)

def _layernorm(x, axis=-1, eps=1e-05):
    m = jnp.mean(x, axis=axis, keepdims=True)
    v = jnp.var(x, axis=axis, keepdims=True)
    return (x - m) / jnp.sqrt(v + eps)

def _scatter_add(tgt, idx, src, axis=0):
    return tgt.at[idx].add(src)

def _segment_sum(src, seg, n):
    return jax.ops.segment_sum(src, seg, n)
kernel_name = 'mk_flamingo_gated_d1_seqx_r8_9b323c'

def setup_inputs(seed: int=0):
    np.random.seed(seed)
    _w = jnp.asarray

    def _rec_inputs():
        import jax
        import jax.numpy as jnp
        _rk = jax.random.key(seed)
        x = 0.002226 + 0.9996 * jax.random.normal(jax.random.fold_in(_rk, 1), (32, 64, 128), jnp.float32)
        _lenS = 64 - jax.random.randint(jax.random.fold_in(_rk, 7), (32,), 0, max(1, 64 // 4) + 1, jnp.int32)
        _lenS2 = 64 - jax.random.randint(jax.random.fold_in(_rk, 8), (32,), 0, max(1, 64 // 4) + 1, jnp.int32)
        _ctx_1024P = jax.random.normal(jax.random.fold_in(_rk, 11), (32, 16, 128), jnp.float32)
        _ctx_1024c = jax.random.dirichlet(jax.random.fold_in(_rk, 511), 0.3 * jnp.ones((16,), jnp.float32), (32, 64))
        _ctx_1024t = jnp.einsum('bsk,bkd->bsd', _ctx_1024c, _ctx_1024P)
        _ctx_1024t = _ctx_1024t * jax.lax.rsqrt(jnp.mean(jnp.square(_ctx_1024t)) + 1e-12) * 0.953939
        ctx_1024 = -0.000125008 + 0.999885 * (_ctx_1024t + 0.3 * jax.random.normal(jax.random.fold_in(_rk, 611), (32, 64, 128), jnp.float32))
        _validS = jnp.arange(64)[None, :] < _lenS[:, None]
        _validS2 = jnp.arange(64)[None, :] < _lenS2[:, None]
        _causal = jnp.tril(jnp.ones((64, 64), dtype=bool))
        mask_BxS2_bk0 = jnp.logical_not(jnp.broadcast_to(_validS2[:, :], (32, 64)))
        _g = jax.random.normal(jax.random.fold_in(_rk, 9001), (2, 1), jnp.float32)
        _g = jnp.sign(_g) * jnp.maximum(jnp.abs(_g), 1.0) + (_g == 0) * 1.0
        g_xattn = _g[0]
        g_ffn = _g[1]
        return (x, ctx_1024, mask_BxS2_bk0, g_xattn, g_ffn)
    x, ctx_1024, mask_BxS2_bk0, g_xattn, g_ffn = _rec_inputs()

    def _L0_xattn_setup():
        import jax, jax.numpy as jnp
        import numpy as np
        EPS = 1e-05

        def layer_norm(x, g, b):
            mu = jnp.mean(x, axis=-1, keepdims=True)
            var = jnp.mean((x - mu) ** 2, axis=-1, keepdims=True)
            return (x - mu) * jax.lax.rsqrt(var + EPS) * g + b
        key = jax.random.key(seed)
        ks = jax.random.split(key, 8)
        b, n, l, D = (8, 512, 64, 128)
        heads, dim_head = (16, 64)
        inner = heads * dim_head
        x = jax.random.normal(ks[0], (b, n, D), dtype=jnp.float32)
        latents = jax.random.normal(ks[1], (b, l, D), dtype=jnp.float32)
        mask = jax.random.randint(ks[2], (b, n), 0, 2) > 0
        Wq = jax.random.normal(ks[3], (D, inner), dtype=jnp.float32) * D ** (-0.5)
        Wkv = jax.random.normal(ks[4], (D, 2 * inner), dtype=jnp.float32) * D ** (-0.5)
        Wout = jax.random.normal(ks[5], (inner, D), dtype=jnp.float32) * inner ** (-0.5)
        g1 = jnp.ones((D,), jnp.float32)
        b1 = jnp.zeros((D,), jnp.float32)
        g2 = jnp.ones((D,), jnp.float32)
        b2 = jnp.zeros((D,), jnp.float32)
        return {'x': x, 'latents': latents, 'mask': mask, 'g1': g1, 'b1': b1, 'g2': g2, 'b2': b2, 'Wq': Wq, 'Wkv': Wkv, 'Wout': Wout}
    _L0_xattn_all = _L0_xattn_setup()
    _L0_xattn_in = {k: v for k, v in _L0_xattn_all.items() if k in ('g1', 'b1', 'g2', 'b2', 'Wq', 'Wkv', 'Wout')}
    del _L0_xattn_all

    def _L0_ffn_setup():
        import jax, jax.numpy as jnp
        import numpy as np
        TOP_K = 2
        CAPACITY_FACTOR = 1.25

        def _moe_forward(x, gate_w, wi_gate, wi_up, wo):
            B, S, D = x.shape
            E = wi_gate.shape[0]
            N = B * S
            capacity = max(int(N / E * CAPACITY_FACTOR), 1)
            x_flat = x.reshape(N, D)
            router_logits = x_flat @ gate_w.T
            router_probs = jax.nn.softmax(router_logits, axis=-1)
            top_k_probs, top_k_idx = jax.lax.top_k(router_probs, TOP_K)
            top_k_probs = top_k_probs / jnp.sum(top_k_probs, axis=-1, keepdims=True)
            out = jnp.zeros_like(x_flat)
            experts = jnp.arange(E, dtype=jnp.int32)
            for k in range(TOP_K):
                eid = top_k_idx[:, k]
                ew = top_k_probs[:, k]
                onehot = (eid[:, None] == experts[None, :]).astype(jnp.int32)
                pos_all = jnp.cumsum(onehot, axis=0) - 1
                pos = jnp.take_along_axis(pos_all, eid[:, None].astype(jnp.int32), axis=1)[:, 0]
                valid = pos < capacity
                pos_c = jnp.where(valid, pos, 0)
                disp = jnp.zeros((E, capacity, D), x_flat.dtype).at[eid, pos_c].add(jnp.where(valid[:, None], x_flat, 0.0))
                gate = jax.nn.silu(jnp.einsum('ecd,efd->ecf', disp, wi_gate))
                up = jnp.einsum('ecd,efd->ecf', disp, wi_up)
                expert_out = jnp.einsum('ecf,edf->ecd', gate * up, wo)
                tok_out = expert_out[eid, pos_c]
                out = out + jnp.where(valid[:, None], ew[:, None] * tok_out, 0.0)
            return out.reshape(B, S, D)
        key = jax.random.key(seed)
        k1, k2, k3, k4, k5 = jax.random.split(key, 5)
        B, S, D, F, E = (4, 256, 128, 512, 8)
        return {'x': jax.random.normal(k1, (B, S, D), dtype=jnp.float32), 'gate_w': jax.random.normal(k2, (E, D), dtype=jnp.float32) * 0.02, 'wi_gate': jax.random.normal(k3, (E, F, D), dtype=jnp.float32) * 0.02, 'wi_up': jax.random.normal(k4, (E, F, D), dtype=jnp.float32) * 0.02, 'wo': jax.random.normal(k5, (E, D, F), dtype=jnp.float32) * 0.02}
    _L0_ffn_all = _L0_ffn_setup()
    _L0_ffn_in = {k: v for k, v in _L0_ffn_all.items() if k in ('gate_w', 'wi_gate', 'wi_up', 'wo')}
    del _L0_ffn_all
    return {'x': x, 'ctx_1024': ctx_1024, 'mask_BxS2_bk0': mask_BxS2_bk0, 'g_xattn': g_xattn, 'g_ffn': g_ffn, 'L0_xattn_g1': _L0_xattn_in['g1'], 'L0_xattn_b1': _L0_xattn_in['b1'], 'L0_xattn_g2': _L0_xattn_in['g2'], 'L0_xattn_b2': _L0_xattn_in['b2'], 'L0_xattn_Wq': _L0_xattn_in['Wq'], 'L0_xattn_Wkv': _L0_xattn_in['Wkv'], 'L0_xattn_Wout': _L0_xattn_in['Wout'], 'L0_ffn_gate_w': _L0_ffn_in['gate_w'], 'L0_ffn_wi_gate': _L0_ffn_in['wi_gate'], 'L0_ffn_wi_up': _L0_ffn_in['wi_up'], 'L0_ffn_wo': _L0_ffn_in['wo']}

def reference(x, ctx_1024, mask_BxS2_bk0, g_xattn, g_ffn, L0_xattn_g1, L0_xattn_b1, L0_xattn_g2, L0_xattn_b2, L0_xattn_Wq, L0_xattn_Wkv, L0_xattn_Wout, L0_ffn_gate_w, L0_ffn_wi_gate, L0_ffn_wi_up, L0_ffn_wo):
    import jax
    import jax.numpy as jnp

    def _L0_xattn_ref(x, latents, mask, g1, b1, g2, b2, Wq, Wkv, Wout):
        import jax, jax.numpy as jnp
        import numpy as np
        EPS = 1e-05

        def layer_norm(x, g, b):
            mu = jnp.mean(x, axis=-1, keepdims=True)
            var = jnp.mean((x - mu) ** 2, axis=-1, keepdims=True)
            return (x - mu) * jax.lax.rsqrt(var + EPS) * g + b
        heads, dim_head = (16, 64)
        b, n, D = x.shape
        l = latents.shape[1]
        xn = layer_norm(x, g1, b1)
        ln_lat = layer_norm(latents, g2, b2)
        q = ln_lat @ Wq
        kv = jnp.concatenate([xn, ln_lat], axis=1) @ Wkv
        k, v = jnp.split(kv, 2, axis=-1)

        def to_heads(t):
            return t.reshape(t.shape[0], t.shape[1], heads, dim_head).transpose(0, 2, 1, 3)
        q, k, v = (to_heads(q), to_heads(k), to_heads(v))
        scale = 1.0 / np.sqrt(np.sqrt(dim_head)).astype(np.float32)
        weight = jnp.einsum('bhld,bhnd->bhln', q * scale, k * scale)
        full_mask = jnp.concatenate([mask, jnp.ones((b, l), dtype=bool)], axis=1)
        neg = -jnp.finfo(weight.dtype).max
        weight = jnp.where(full_mask[:, None, None, :], weight, neg)
        weight = jax.nn.softmax(weight.astype(jnp.float32), axis=-1).astype(q.dtype)
        out = jnp.einsum('bhln,bhnd->bhld', weight, v)
        out = out.transpose(0, 2, 1, 3).reshape(b, l, heads * dim_head)
        return out @ Wout

    def _L0_ffn_ref(x, gate_w, wi_gate, wi_up, wo):
        import jax, jax.numpy as jnp
        import numpy as np
        TOP_K = 2
        CAPACITY_FACTOR = 1.25

        def _moe_forward(x, gate_w, wi_gate, wi_up, wo):
            B, S, D = x.shape
            E = wi_gate.shape[0]
            N = B * S
            capacity = max(int(N / E * CAPACITY_FACTOR), 1)
            x_flat = x.reshape(N, D)
            router_logits = x_flat @ gate_w.T
            router_probs = jax.nn.softmax(router_logits, axis=-1)
            top_k_probs, top_k_idx = jax.lax.top_k(router_probs, TOP_K)
            top_k_probs = top_k_probs / jnp.sum(top_k_probs, axis=-1, keepdims=True)
            out = jnp.zeros_like(x_flat)
            experts = jnp.arange(E, dtype=jnp.int32)
            for k in range(TOP_K):
                eid = top_k_idx[:, k]
                ew = top_k_probs[:, k]
                onehot = (eid[:, None] == experts[None, :]).astype(jnp.int32)
                pos_all = jnp.cumsum(onehot, axis=0) - 1
                pos = jnp.take_along_axis(pos_all, eid[:, None].astype(jnp.int32), axis=1)[:, 0]
                valid = pos < capacity
                pos_c = jnp.where(valid, pos, 0)
                disp = jnp.zeros((E, capacity, D), x_flat.dtype).at[eid, pos_c].add(jnp.where(valid[:, None], x_flat, 0.0))
                gate = jax.nn.silu(jnp.einsum('ecd,efd->ecf', disp, wi_gate))
                up = jnp.einsum('ecd,efd->ecf', disp, wi_up)
                expert_out = jnp.einsum('ecf,edf->ecd', gate * up, wo)
                tok_out = expert_out[eid, pos_c]
                out = out + jnp.where(valid[:, None], ew[:, None] * tok_out, 0.0)
            return out.reshape(B, S, D)
        return _moe_forward(x, gate_w, wi_gate, wi_up, wo)
    x = x + jnp.tanh(g_xattn[0]) * _L0_xattn_ref(ctx_1024, _layernorm(x, axis=-1), mask_BxS2_bk0, L0_xattn_g1, L0_xattn_b1, L0_xattn_g2, L0_xattn_b2, L0_xattn_Wq, L0_xattn_Wkv, L0_xattn_Wout)
    x = x + jnp.tanh(g_ffn[0]) * _L0_ffn_ref(_layernorm(x, axis=-1), L0_ffn_gate_w, L0_ffn_wi_gate, L0_ffn_wi_up, L0_ffn_wo)
    return x

_drawn_inputs = setup_inputs


def setup_inputs(seed=0):
    import zlib

    import numpy as np

    out = dict(_drawn_inputs(seed))
    spreads = {'L0_xattn_g1': (1.0, 0.6),
     'L0_xattn_b1': (0.0, 0.787),
     'L0_xattn_g2': (1.0, 0.2),
     'L0_xattn_b2': (0.0, 0.1)}
    factors = {'L0_ffn_gate_w': 8.0, 'L0_ffn_wi_gate': 7.395, 'L0_ffn_wi_up': 7.35, 'L0_ffn_wo': 7.351}
    for name, (base, spread) in spreads.items():
        noise = np.random.default_rng([zlib.crc32(name.encode()), seed]).standard_normal(out[name].shape)
        drawn = base * np.exp(spread * noise) if base else spread * noise
        out[name] = jnp.asarray(drawn.astype(out[name].dtype))
    for name, factor in factors.items():
        out[name] = (out[name] * factor).astype(out[name].dtype)
    return out
```

```python
from contextlib import ExitStack

import concourse.bass as bass
from concourse import mybir

F32 = mybir.dt.float32
BF16 = mybir.dt.bfloat16
U32 = mybir.dt.uint32
I32 = mybir.dt.int32
U8 = mybir.dt.uint8
ALU = mybir.AluOpType
ACT = mybir.ActivationFunctionType
AX_X = mybir.AxisListType.X

P = 128
B, S, D = 32, 64, 128
HEADS, DH = 16, 64
EPS = 1e-5
E, F = 8, 512
TOP_K = 2
N = B * S
CAP = max(int(N / E * 1.25), 1)
ROWS = TOP_K * CAP
SLOTS = E * ROWS
SCALE = 1.0 / float(DH) ** 0.5
MASKED = 1e30

GB = 4
NG = B // GB
HALVES = 2 * GB
PAIRS = 4
GT = GB * S
TC = GT // P
FC = F // P
SC = ROWS // P
NT = N // P
assert ROWS % P == 0 and CAP <= 512 and NG % 2 == 0


def flamingo_block(nc, x, ctx_in, mask, g_xattn, g_ffn, g1, b1, g2, b2, Wq, Wkv, Wout,
                   gate_w, wi_gate, wi_up, wo, out):
    with ExitStack() as ctx:
        def sb(name, shape, dt=F32):
            return ctx.enter_context(nc.sbuf_tensor(name, shape, dt))

        def bank(name):
            return ctx.enter_context(nc.psum_tensor(name, [P, 512], F32))

        def sem(name):
            return ctx.enter_context(nc.semaphore(name))

        x_flat = x.rearrange("b s d -> (b s) d")
        out_flat = out.rearrange("b s d -> (b s) d")
        x_slots = nc.dram_tensor("x_slots", (SLOTS, D), F32).ap()
        y_slots = nc.dram_tensor("y_slots", (SLOTS + 1, D), F32).ap()

        ident = sb("ident", [P, P])
        before = sb("before", [P, P], BF16)
        ones = sb("ones", [P, P], BF16)
        iota_i = sb("iota_i", [P, E], I32)
        iota_e = sb("iota_e", [P, E])
        k_offset = sb("k_offset", [P, TC * TOP_K])
        minus_half = sb("minus_half", [P, GB])
        var_scale = sb("var_scale", [P, 1])
        var_eps = sb("var_eps", [P, 1])
        zeros = sb("zeros", [P, SC * D])
        wq_sb = sb("wq_sb", [P, HEADS * DH])
        wkv_sb = sb("wkv_sb", [P, 2 * HEADS * DH])
        wout_sb = sb("wout_sb", [P, HEADS // 2, D])
        gate_sb = sb("gate_sb", [E, D])
        gate_t = sb("gate_t", [P, E])
        affine = sb("affine", [P, 2, D])
        mask_u8 = sb("mask_u8", [1, N], U8)
        mask_add = sb("mask_add", [1, N], BF16)
        gains = sb("gains", [P, 2])
        tanhs = sb("tanhs", [P, 2])
        w_t = sb("w_t", [P, 3 * HEADS // 2, P])
        A = sb("A", [P, HEADS, D])
        Bw = sb("Bw", [P, HEADS, D])
        raw = sb("raw", [P, 2, GB, D])
        normed = sb("normed", [P, 2, GB, D])
        scaled = sb("scaled", [P, GB, D])
        X = sb("X", [P, 2, GB, D])
        XT = sb("XT", [P, 2, GB, P])
        stats = sb("stats", [P, GB, 6])
        moments = sb("moments", [P, GB, 2])
        var_adj = sb("var_adj", [P, GB])
        rstd = sb("rstd", [P, GB])
        q = sb("q", [P, 2, GB, HEADS, S])
        mask_g = sb("mask_g", [1, 2, GB, S], BF16)
        neg_max = sb("neg_max", [P, 4, PAIRS])
        sums = sb("sums", [P, 4, PAIRS])
        rsums = sb("rsums", [P, 4, PAIRS])
        probs = sb("probs", [P, 4, PAIRS, P])
        probs_t = sb("probs_t", [P, 2, 512])
        px = sb("px", [P, 2, GB, HEADS, S])
        yt = sb("yt", [P, TC, P])
        resid = sb("resid", [P, 2, TC, D])
        x1 = sb("x1", [P, 2, TC, D])
        x1_all = sb("x1_all", [P, NT, D])
        t_stats = sb("t_stats", [P, TC, 6])
        t_moments = sb("t_moments", [P, TC, 2])
        t_var = sb("t_var", [P, TC])
        t_rstd = sb("t_rstd", [P, TC])
        xn = sb("xn", [P, 2, TC, D])
        xn_t = sb("xn_t", [P, TC, P])
        logits = sb("logits", [P, TC, E])
        top = sb("top", [P, TC, 8])
        top_i = sb("top_i", [P, TC, 8], U32)
        choice = sb("choice", [P, TC * TOP_K])
        onehot = sb("onehot", [P, TC * TOP_K, E], BF16)
        counts = sb("counts", [P, TOP_K * E], BF16)
        placed = sb("placed", [P, TC * TOP_K, E])
        pos = sb("pos", [P, TC * TOP_K])
        base = sb("base", [P, TC * TOP_K])
        valid = sb("valid", [P, TC * TOP_K])
        moved = sb("moved", [P, TC * TOP_K])
        slot = sb("slot", [P, 2, TC * TOP_K], U32)
        slot_all = sb("slot_all", [P, NT, TOP_K], U32)
        gap = sb("gap", [P, TC])
        ratio = sb("ratio", [P, TC])
        ratio1 = sb("ratio1", [P, TC])
        wts = sb("wts", [P, TC, TOP_K])
        wts_g = sb("wts_g", [P, TC, TOP_K])
        wts_all = sb("wts_all", [P, NT, TOP_K])
        ew = sb("ew", [P, 2, 3, FC, P])
        ewt = sb("ewt", [P, 2, 3, FC, P])
        xe = sb("xe", [P, 2, SC, D])
        xe_t = sb("xe_t", [P, 2, SC * P])
        silu = sb("silu", [P, 2, CAP])
        hid = q[:].rearrange("p a b h s -> p a (b h s)")[:, :, 0:FC * ROWS].rearrange("p a (f r) -> p a f r", f=FC)
        ye = px[:].rearrange("p a b h s -> p a (b h s)")[:, :, 0:SC * D].rearrange("p a (c d) -> p a c d", c=SC)
        y_pick = w_t[:, 0:4 * TOP_K].rearrange("p (r k) d -> p r k d", k=TOP_K)
        pick_i = sb("pick_i", [P, 4, TOP_K], U32)
        part = w_t[:, 8:12]
        final = w_t[:, 12:16]

        sc_bank = [bank("sc0"), bank("sc1")]
        tr_bank = bank("tr")
        px_bank = bank("pxb")
        q_bank = [bank("q0"), bank("q1")]
        y_bank = bank("yb")
        r_bank = bank("rb")
        setup_banks = [sc_bank[0], sc_bank[1], tr_bank, px_bank, q_bank[0], q_bank[1]]

        in_qkv, in_wout, in_small, in_gate = sem("in_qkv"), sem("in_wout"), sem("in_small"), sem("in_gate")
        in_raw = [sem("in_raw0"), sem("in_raw1")]
        in_resid = [sem("in_resid0"), sem("in_resid1")]
        zeroed, slots_zeroed = sem("zeroed"), sem("slots_zeroed")
        const_step, consts = sem("const_step"), sem("consts")
        small_done, tanh_done = sem("small_done"), sem("tanh_done")
        wt_done, wt_copied = sem("wt_done"), sem("wt_copied")
        ab_done, ab_copied = sem("ab_done"), sem("ab_copied")
        gate_done = sem("gate_done")
        stats_step, rstd_step = sem("stats_step"), sem("rstd_step")
        normed_done, scaled_done, X_done = sem("normed_done"), sem("scaled_done"), sem("X_done")
        xt_done, xt_copied = sem("xt_done"), sem("xt_copied")
        q_done, q_copied_dve, q_copied_act = sem("q_done"), sem("q_copied_dve"), sem("q_copied_act")
        mask_ready = sem("mask_ready")
        s_done, max_done, exp_done = sem("s_done"), sem("max_done"), sem("exp_done")
        recip_done, norm_done = sem("recip_done"), sem("norm_done")
        tr_done, tr_copied = sem("tr_done"), sem("tr_copied")
        px_done, px_copied = sem("px_done"), sem("px_copied")
        y_done, y_copied, yt_done = sem("y_done"), sem("y_copied"), sem("yt_done")
        x1_done, t_stats_step, t_rstd_step = sem("x1_done"), sem("t_stats_step"), sem("t_rstd_step")
        xn_done, xnt_done, xnt_copied = sem("xn_done"), sem("xnt_done"), sem("xnt_copied")
        logits_done, route_step = sem("logits_done"), sem("route_step")
        gap_done, ratio_done, wts_done = sem("gap_done"), sem("ratio_done"), sem("wts_done")
        onehot_done, pos_done, counts_step = sem("onehot_done"), sem("pos_done"), sem("counts_step")
        place_step, slot_done = sem("place_step"), sem("slot_done")
        x1_kept = [sem("x1_kept0"), sem("x1_kept1")]
        wts_kept, slot_kept = sem("wts_kept"), sem("slot_kept")
        scattered, xn_free = [sem("scattered0"), sem("scattered1")], sem("xn_free")
        in_ew = [sem("in_ew0"), sem("in_ew1")]
        in_xe = [sem("in_xe0"), sem("in_xe1")]
        ewt_done, ewt_copied = sem("ewt_done"), sem("ewt_copied")
        xet_done, xet_copied = sem("xet_done"), sem("xet_copied")
        gu_done, silu_done, hid_done = sem("gu_done"), sem("silu_done"), sem("hid_done")
        ye_done, ye_copied = sem("ye_done"), sem("ye_copied")
        y_stored = [sem("y_stored0"), sem("y_stored1")]
        pick_ready = sem("pick_ready")
        picked = [sem(f"picked{r}") for r in range(4)]
        waits_met = sem("waits_met")
        part_done, final_done = sem("part_done"), sem("final_done")
        stored = [sem(f"stored{r}") for r in range(4)]

        def apart(eng):
            eng.sem_inc(waits_met, 1)

        def schedule(eng, body):
            body(0, 0, 0, True, False)
            with eng.Fori(0, NG // 2 - 1) as it:
                body(it * 2 + 1, 1, it, False, False)
                body(it * 2 + 2, 0, it + 1, False, False)
            body(NG - 1, 1, NG // 2 - 1, False, True)

        block = ctx.enter_context(nc.Block())

        @block.sync
        def _(sp):
            def load_raw(n, p):
                sp.dma_start(raw[0:S, p], ctx_in[bass.ds(n * GB, GB)].rearrange("b s d -> s b d")).then_inc(in_raw[p], 16)
                sp.dma_start(raw[S:P, p], x[bass.ds(n * GB, GB)].rearrange("b s d -> s b d")).then_inc(in_raw[p], 16)

            def load_resid(n, p):
                sp.dma_start(resid[:, p], x_flat[bass.ds(n * GT, GT), :].rearrange("(c p) d -> p c d", p=P)
                             ).then_inc(in_resid[p], 16)

            load_raw(0, 0)
            sp.dma_start(wq_sb[:], Wq).then_inc(in_qkv, 16)
            sp.dma_start(wkv_sb[:], Wkv).then_inc(in_qkv, 16)
            sp.dma_start(wout_sb[:], Wout.rearrange("(c p) e -> p c e", p=P)).then_inc(in_wout, 16)
            load_raw(1, 1)
            load_resid(0, 0)
            load_resid(1, 1)
            sp.wait_ge(zeroed, 1)
            for e in range(E):
                sp.dma_start(x_slots[e * ROWS:(e + 1) * ROWS, :].rearrange("(p c) d -> p (c d)", p=P),
                             zeros[:]).then_inc(slots_zeroed, 16)
            sp.dma_start(y_slots[SLOTS:SLOTS + 1, :], zeros[0:1, 0:D]).then_inc(slots_zeroed, 16)

            def load_expert(e, p):
                for j, w in enumerate((wi_gate, wi_up)):
                    sp.dma_start(ew[:, p, j], w[bass.ds(e, 1)].rearrange("o (c p) d -> p (o c) d", p=P)
                                 ).then_inc(in_ew[p], 16)
                sp.dma_start(ew[:, p, 2], wo[bass.ds(e, 1)].rearrange("o d (c f) -> d (o c) f", c=FC)
                             ).then_inc(in_ew[p], 16)

            load_expert(0, 0)
            load_expert(1, 1)
            sp.wait_ge(normed_done, 1)
            load_raw(2, 0)

            def next_group(n, p, nh, more=True):
                if more:
                    sp.wait_ge(normed_done, n)
                    load_raw(n + 1, 1 - p)
                sp.wait_ge(x1_done, n - 1)
                load_resid(n, p)
                sp.wait_ge(scattered[p], nh * 16 * TC * TOP_K)
                sp.sem_inc(xn_free, 1)

            with sp.Fori(1, NG // 2 - 1) as it:
                next_group(it * 2, 0, it)
                next_group(it * 2 + 1, 1, it)
            next_group(NG - 2, 0, NG // 2 - 1)
            next_group(NG - 1, 1, NG // 2 - 1, more=False)

            def load_inputs(e, p):
                sp.dma_start(xe[:, p], x_slots[bass.ds(e * ROWS, ROWS), :].rearrange("(c p) d -> p c d", p=P)
                             ).then_inc(in_xe[p], 16)

            def store_outputs(e, p):
                sp.wait_ge(ye_copied, e * 2 + 2)
                sp.dma_start(y_slots[bass.ds(e * ROWS, ROWS), :].rearrange("(c p) d -> p c d", p=P), ye[:, p]
                             ).then_inc(y_stored[p], 16)

            for p in range(2):
                sp.wait_ge(scattered[p], 16 * TOP_K * NT // 2)
            load_inputs(0, 0)
            load_inputs(1, 1)

            def expert_io(e, p, more):
                if more:
                    sp.wait_ge(ewt_done, e * 3 + 3)
                    load_expert(e + 2, p)
                    sp.wait_ge(xet_done, e * 2 + 2)
                    load_inputs(e + 2, p)
                store_outputs(e, p)

            with sp.Fori(0, E // 2 - 1) as it:
                expert_io(it * 2, 0, True)
                expert_io(it * 2 + 1, 1, True)
            expert_io(E - 2, 0, False)
            expert_io(E - 1, 1, False)

            def store_final(c, r):
                sp.wait_ge(final_done, c + 1)
                sp.dma_start(out_flat[bass.ds(c * P, P), :], final[:, r]).then_inc(stored[r], 16)

            with sp.Fori(0, NT // 4) as it:
                for r in range(4):
                    store_final(it * 4 + r, r)
            for r in range(4):
                sp.wait_ge(stored[r], 16 * NT // 4)

        @block.gpsimd
        def _(pool):
            count = [0]

            def const(ins):
                ins.then_inc(const_step, 1)
                count[0] += 1

            for s in (*x1_kept, wts_kept, slot_kept, counts_step, y_copied):
                pool.sem_inc(s, 1)
            pool.sem_inc(xn_free, 2)
            for j, g in enumerate((g1, b1)):
                pool.dma_start(affine[0:S, j], g.partition_broadcast(S)).then_inc(in_small, 16)
            for j, g in enumerate((g2, b2)):
                pool.dma_start(affine[S:P, j], g.partition_broadcast(S)).then_inc(in_small, 16)
            const(pool.memset(ident[:], 0.0))
            const(pool.memset(before[:], 0.0))
            pool.wait_ge(const_step, 2)
            const(pool.affine_select(out=ident[:], in_=ident[:], compare_op=ALU.not_equal, fill=1.0, base=0,
                                     pattern=[[-1, P]], channel_multiplier=1))
            const(pool.affine_select(out=before[:], in_=before[:], compare_op=ALU.is_ge, fill=1.0, base=0,
                                     pattern=[[-1, P]], channel_multiplier=1))
            const(pool.memset(ones[:], 1.0))
            const(pool.memset(counts[:], 0.0))
            const(pool.memset(minus_half[:], -0.5))
            const(pool.iota(iota_i[:], [[1, E]], base=0, channel_multiplier=0))
            for k in range(TC * TOP_K):
                const(pool.memset(k_offset[:, k:k + 1], float(k % TOP_K * CAP)))
            const(pool.memset(var_scale[0:S], 1.0))
            const(pool.memset(var_eps[0:S], EPS))
            pool.wait_ge(const_step, count[0])
            const(pool.memset(var_scale[S:P], 1.0 + EPS))
            const(pool.memset(var_eps[S:P], EPS * EPS))
            pool.wait_ge(const_step, count[0])
            pool.tensor_copy(iota_e[:], iota_i[:]).then_inc(consts, 1)
            pool.memset(zeros[:], 0.0).then_inc(zeroed, 1)

            def ln_rstd(n):
                pool.wait_ge(stats_step, n * 2 * GB + 2 * GB)
                apart(pool)
                pool.tensor_scalar(var_adj[:], moments[:, :, 1], var_scale[:, 0:1], var_eps[:, 0:1],
                                   ALU.mult, ALU.add).then_inc(rstd_step, 1)
                pool.wait_ge(rstd_step, n * 2 + 1)
                pool.tensor_tensor(rstd[:], var_adj[:], minus_half[:], ALU.pow).then_inc(rstd_step, 1)

            def ln_affine(n, p, first):
                pool.wait_ge(normed_done, n + 1)
                if first:
                    pool.wait_ge(in_small, 4 * 16)
                pool.tensor_tensor(scaled[:], normed[:, p], affine[:, 0:1, :].broadcast_to((P, GB, D)),
                                   ALU.mult).then_inc(scaled_done, 1)
                if not first:
                    pool.wait_ge(px_done, (n - 1) * HALVES)
                pool.wait_ge(scaled_done, n + 1)
                pool.tensor_tensor(X[:, p], scaled[:], affine[:, 1:2, :].broadcast_to((P, GB, D)),
                                   ALU.add).then_inc(X_done, 1)

            def group_mask(n, p):
                pool.tensor_copy(mask_g[:, p].rearrange("a b s -> a (b s)"), mask_add[0:1, bass.ds(n * GT, GT)]
                                 ).then_inc(mask_ready, 1)

            ln_rstd(0)
            ln_affine(0, 0, True)
            pool.wait_ge(small_done, 1)
            group_mask(0, 0)

            def normalise(u, r):
                pool.wait_ge(recip_done, u + 1)
                pool.tensor_tensor(probs[:, r], probs[:, r],
                                   rsums[:, r].unsqueeze(2).broadcast_to((P, PAIRS, P)), ALU.mult
                                   ).then_inc(norm_done, 1)

            def token_rstd(n):
                pool.wait_ge(t_stats_step, n * 2 * TC + 2 * TC)
                apart(pool)
                pool.tensor_scalar(t_var[:], t_moments[:, :, 1], EPS, None, ALU.add).then_inc(t_rstd_step, 1)
                pool.wait_ge(t_rstd_step, n * 2 + 1)
                pool.tensor_tensor(t_rstd[:], t_var[:], minus_half[:, 0:TC], ALU.pow).then_inc(t_rstd_step, 1)

            def count_tokens(n):
                pool.wait_ge(pos_done, n + 1)
                for c in range(TC):
                    pool.tensor_tensor(counts[:], counts[:], onehot[:, TOP_K * c:TOP_K * (c + 1), :].rearrange(
                        "p k e -> p (k e)"), ALU.add).then_inc(counts_step, 1)
                    pool.wait_ge(counts_step, n * TC + c + 2)

            def keep_and_scatter(n, p):
                pool.tensor_copy(x1_all[:, bass.ds(n * TC, TC), :], x1[:, p]).then_inc(x1_kept[p], 1)
                pool.wait_ge(wts_done, n + 1)
                pool.tensor_copy(wts_all[:, bass.ds(n * TC, TC), :], wts_g[:]).then_inc(wts_kept, 1)
                pool.wait_ge(slot_done, n + 1)
                pool.tensor_copy(slot_all[:, bass.ds(n * TC, TC), :].rearrange("p c k -> p (c k)"), slot[:, p]
                                 ).then_inc(slot_kept, 1)
                for c in range(TC):
                    for k in range(TOP_K):
                        i = TOP_K * c + k
                        pool.indirect_dma_start(x_slots, bass.IndirectOffsetOnAxis(slot[:, p, i:i + 1], 0),
                                                xn[:, p, c], None, bounds_check=SLOTS - 1, oob_is_err=False
                                                ).then_inc(scattered[p], 16)

            def tail_a(n, p):
                pool.wait_ge(x1_done, n + 1)
                token_rstd(n)

            def tail_b(n, p):
                count_tokens(n)
                keep_and_scatter(n, p)

            pool.wait_ge(slots_zeroed, 16 * (E + 1))

            def group(g, p, gh, first, last):
                for i in range(HALVES):
                    if i == 1 and not last:
                        ln_rstd(g + 1)
                    normalise(g * HALVES + i, i % 4)
                    if i == 3 and not last:
                        ln_affine(g + 1, 1 - p, first=False) if not first else ln_affine(1, 1, True)
                        group_mask(g + 1, 1 - p)
                    if i == 5 and not first:
                        tail_a(g - 1, 1 - p)
                if not first:
                    tail_b(g - 1, 1 - p)

            schedule(pool, group)
            tail_a(NG - 1, 1)
            tail_b(NG - 1, 1)

            for p in range(2):
                pool.wait_ge(y_stored[p], 16 * E // 2)
            pool.wait_ge(slot_kept, NG + 1)

            def fetch(c, r, again):
                if again:
                    pool.wait_ge(final_done, c - 3)
                pool.tensor_copy(pick_i[:, r], slot_all[:, bass.ds(c, 1), :].rearrange("p c k -> p (c k)")
                                 ).then_inc(pick_ready, 1)
                pool.wait_ge(pick_ready, c + 1)
                apart(pool)
                for k in range(TOP_K):
                    pool.indirect_dma_start(y_pick[:, r, k], None, y_slots,
                                            bass.IndirectOffsetOnAxis(pick_i[:, r, k:k + 1], 0)
                                            ).then_inc(picked[r], 16)

            for r in range(4):
                fetch(r, r, False)
            with pool.Fori(1, NT // 4) as it:
                for r in range(4):
                    fetch(it * 4 + r, r, True)

        @block.scalar
        def _(act):
            act.dma_start(gains[:, 0:1], g_xattn.partition_broadcast(P)).then_inc(in_gate, 16)
            act.dma_start(gains[:, 1:2], g_ffn.partition_broadcast(P)).then_inc(in_gate, 16)
            act.dma_start(gate_sb[:], gate_w).then_inc(in_gate, 16)
            act.dma_start(mask_u8[:], mask.rearrange("b s -> (b s)").unsqueeze(0)).then_inc(in_gate, 16)
            act.wait_ge(in_gate, 64)
            act.activation(tanhs[:], gains[:], ACT.Tanh).then_inc(tanh_done, 1)
            for k in range(6):
                act.wait_ge(wt_done, k + 1)
                act.copy(w_t[:, 4 * k:4 * k + 4].rearrange("p c m -> p (c m)"), setup_banks[k][:]
                         ).then_inc(wt_copied, 1)

            def q_copy(n, p, k):
                act.wait_ge(q_done, n * 8 + k + 1)
                act.copy(q[:, p, :, 2 * k:2 * k + 2, :].rearrange("p b h s -> p h b s"),
                         q_bank[k % 2][:].rearrange("p (h b s) -> p h b s", h=2, b=GB)
                         ).then_inc(q_copied_act, 1)

            for k in range(1, 8, 2):
                q_copy(0, 0, k)

            def softmax(u, i, early):
                r = i % 4
                act.wait_ge(max_done, u + 1)
                if not early:
                    act.wait_ge(tr_done, u - 3)
                for j in range(PAIRS):
                    act.activation(probs[:, r, j], sc_bank[i % 2][:, j * P:(j + 1) * P], ACT.Exp,
                                   bias=neg_max[:, r, j:j + 1], accum_out=sums[:, r, j:j + 1]
                                   ).then_inc(exp_done, 1)

            def copy_probs(v, i, early):
                act.wait_ge(tr_done, v + 1)
                if not early:
                    act.wait_ge(px_done, v - 1)
                act.copy(probs_t[:, i % 2], tr_bank[:]).then_inc(tr_copied, 1)

            def copy_y(n):
                act.wait_ge(y_done, n + 1)
                act.copy(yt[:].rearrange("p c t -> p (c t)"), y_bank[:, 0:GT]).then_inc(y_copied, 1)

            def copy_xnt(n):
                act.wait_ge(xnt_done, n + 1)
                act.copy(xn_t[:].rearrange("p c t -> p (c t)"), r_bank[:, 0:GT]).then_inc(xnt_copied, 1)

            def gate_ratio(n):
                act.wait_ge(gap_done, n + 1)
                act.activation(ratio[:], gap[:], ACT.Exp).then_inc(ratio_done, 1)

            def group(g, p, gh, first, last):
                for i in range(HALVES):
                    u = g * HALVES + i
                    softmax(u, i, first and i < 4)
                    if not last and i >= 5:
                        for k in {5: (1,), 6: (3, 5), 7: (7,)}[i]:
                            q_copy(g + 1, 1 - p, k)
                    if not (first and i < 2):
                        copy_probs(u - 2, i - 2, first and i < 4)
                    if not first:
                        if i == 4:
                            copy_y(g - 1)
                        if i == 6:
                            copy_xnt(g - 1)
                        if i == 7:
                            gate_ratio(g - 1)

            schedule(act, group)
            U = NG * HALVES
            copy_probs(U - 2, 0, False)
            copy_probs(U - 1, 1, False)
            copy_y(NG - 1)
            copy_xnt(NG - 1)
            gate_ratio(NG - 1)

            def copy_transposed(e, p, i):
                act.wait_ge(ewt_done, e * 3 + i + 1)
                act.copy(ewt[:, p, i].rearrange("p c m -> p (c m)"), (tr_bank, r_bank, tr_bank)[i][:]
                         ).then_inc(ewt_copied, 1)

            def prepare(e, p):
                for i in range(3):
                    copy_transposed(e, p, i)

            def gate(e, p):
                for i in range(2 * FC):
                    n = e * 2 * FC + i
                    act.wait_ge(gu_done, n + 1)
                    act.activation(silu[:, i % 2], sc_bank[i % 2][:, 0:CAP], ACT.Silu).then_inc(silu_done, 1)

            prepare(0, 0)
            prepare(1, 1)

            def expert(e, p, more):
                gate(e, p)
                if more:
                    prepare(e + 2, p)

            with act.Fori(0, E // 2 - 1) as it:
                expert(it * 2, 0, True)
                expert(it * 2 + 1, 1, True)
            expert(E - 2, 0, False)
            expert(E - 1, 1, False)

        @block.tensor
        def _(pe):
            pe.wait_ge(consts, 1)
            pe.wait_ge(in_qkv, 32)
            for k in range(6):
                for j in range(4):
                    c = 4 * k + j
                    src = wq_sb[:, c * P:(c + 1) * P] if c < 8 else wkv_sb[:, (c - 8) * P:(c - 7) * P]
                    mm = pe.transpose(setup_banks[k][:, j * P:(j + 1) * P], src, ident[:])
                mm.then_inc(wt_done, 1)

            def transpose_x(n, p):
                pe.wait_ge(X_done, n + 1)
                for b in range(GB):
                    mm = pe.transpose(r_bank[:, b * P:(b + 1) * P], X[:, p, b], ident[:])
                mm.then_inc(xt_done, 1)

            transpose_x(0, 0)
            pe.wait_ge(in_gate, 64)
            pe.transpose(y_bank[:, 0:E], gate_sb[:], ident[0:E, 0:E]).then_inc(gate_done, 1)
            pe.wait_ge(in_wout, 16)
            for k in range(8):
                if k == 0:
                    pe.wait_ge(wt_copied, 6)
                if k >= 6:
                    pe.wait_ge(ab_copied, k - 5)
                for j in range(4):
                    h = 8 * (k % 4 // 2) + 2 * j + k % 2
                    rows = slice(DH * (h % 2), DH * (h % 2) + DH)
                    if k < 4:
                        lhs, rhs = w_t[rows, h // 2], w_t[rows, 8 + h // 2]
                    else:
                        lhs, rhs = w_t[rows, 16 + h // 2], wout_sb[rows, h // 2]
                    mm = pe.matmul(setup_banks[k % 6][:, j * P:(j + 1) * P], lhs, rhs, start=True, stop=True)
                mm.then_inc(ab_done, 1)

            def project(n, p, h):
                k = h // 2
                if h % 2 == 0:
                    if k >= 2:
                        pe.wait_ge(q_copied_dve if k % 2 == 0 else q_copied_act, n * 4 + k // 2)
                    elif not (isinstance(n, int) and n == 0):
                        pe.wait_ge(q_copied_dve if k % 2 == 0 else q_copied_act, n * 4)
                mm = pe.matmul(q_bank[k % 2][:, (h % 2) * GT:(h % 2 + 1) * GT], A[:, h], XT[:, p, :, S:P],
                               start=True, stop=True)
                if h % 2:
                    mm.then_inc(q_done, 1)

            pe.wait_ge(ab_copied, 8)
            pe.wait_ge(xt_copied, 1)
            for h in range(HEADS):
                project(0, 0, h)

            def scores(g, p, u, i, early):
                b, hf = divmod(i, 2)
                if i == 0:
                    pe.wait_ge(q_copied_dve, g * 4 + 4)
                    pe.wait_ge(q_copied_act, g * 4 + 4)
                    pe.wait_ge(mask_ready, g + 1)
                if not early:
                    pe.wait_ge(exp_done, (u - 1) * PAIRS)
                s = sc_bank[i % 2][:].rearrange("p (j k) -> p j k", j=PAIRS)
                pe.matmul(s[:, :, 0:S], ones[0:1, :], mask_g[:, p, b:b + 1].broadcast_to((1, PAIRS, S)),
                          start=True, stop=False, skip_group_check=True)
                for j in range(PAIRS):
                    h = 2 * (PAIRS * hf + j)
                    mm = pe.matmul(s[:, j], q[:, p, b, h:h + 2].rearrange("p h s -> p (h s)"), XT[:, p, b],
                                   start=False, stop=(j == PAIRS - 1), skip_group_check=True)
                mm.then_inc(s_done, 1)

            def transpose_probs(v, i, early):
                pe.wait_ge(norm_done, v + 1)
                if not early:
                    pe.wait_ge(tr_copied, v)
                for j in range(PAIRS):
                    mm = pe.transpose(tr_bank[:, j * P:(j + 1) * P], probs[:, i % 4, j], ident[:])
                mm.then_inc(tr_done, 1)

            def mix(v, p, i, early):
                pe.wait_ge(tr_copied, v + 1)
                if not early:
                    pe.wait_ge(px_copied, v)
                pe.matmul(px_bank[:], X[:, p, i // 2], probs_t[:, i % 2], start=True, stop=True
                          ).then_inc(px_done, 1)

            def out_heads(n, p, h0, h1):
                if h0 == 0:
                    pe.wait_ge(px_copied, n * HALVES + HALVES)
                    pe.wait_ge(y_copied, n + 1)
                for h in range(h0, h1):
                    mm = pe.matmul(y_bank[:, 0:GT], Bw[:, h], px[:, p, :, h], start=(h == 0),
                                   stop=(h == HEADS - 1))
                if h1 == HEADS:
                    mm.then_inc(y_done, 1)

            def transpose_y(n):
                pe.wait_ge(y_copied, n + 2)
                for c in range(TC):
                    mm = pe.transpose(r_bank[:, c * P:(c + 1) * P], yt[:, c], ident[:])
                mm.then_inc(yt_done, 1)

            def transpose_xn(n, p):
                pe.wait_ge(xn_done, n * TC + TC)
                for c in range(TC):
                    mm = pe.transpose(r_bank[:, c * P:(c + 1) * P], xn[:, p, c], ident[:])
                mm.then_inc(xnt_done, 1)

            def route_logits(n):
                pe.wait_ge(xnt_copied, n + 1)
                for c in range(TC):
                    mm = pe.matmul(r_bank[:, c * E:(c + 1) * E], xn_t[:, c], gate_t[:], start=True, stop=True)
                mm.then_inc(logits_done, 1)

            def positions(n):
                pe.wait_ge(onehot_done, n + 1)
                pe.wait_ge(counts_step, n * TC + 1)
                for c in range(TC):
                    o = r_bank[:, 64 + c * TOP_K * E:64 + (c + 1) * TOP_K * E]
                    hot = [onehot[:, TOP_K * a:TOP_K * (a + 1)].rearrange("p k e -> p (k e)") for a in range(c + 1)]
                    pe.matmul(o, before[:], hot[c], start=True, stop=False)
                    for a in range(c):
                        pe.matmul(o, ones[:], hot[a], start=False, stop=False)
                    mm = pe.matmul(o, ones[:], counts[:], start=False, stop=True)
                mm.then_inc(pos_done, 1)

            def group(g, p, gh, first, last):
                for i in range(HALVES):
                    u = g * HALVES + i
                    if i == 7 and not first:
                        route_logits(g - 1)
                    scores(g, p, u, i, first and i < 2)
                    if i == 4 and not last:
                        transpose_x(g + 1, 1 - p)
                    if not first:
                        if i == 3:
                            out_heads(g - 1, 1 - p, 0, 8)
                        if i == 4:
                            out_heads(g - 1, 1 - p, 8, 16)
                        if i == 5:
                            pe.wait_ge(xt_copied, g + 1 if last else g + 2)
                            transpose_y(g - 1)
                        if i == 6:
                            transpose_xn(g - 1, 1 - p)
                    if not last and i >= 5:
                        if i == 5:
                            pe.wait_ge(xt_copied, g + 2)
                        for h in {5: range(0, 6), 6: range(6, 12), 7: range(12, 16)}[i]:
                            project(g + 1, 1 - p, h)
                    if not (first and i < 2):
                        transpose_probs(u - 2, (i - 2) % 4, first and i == 2)
                    if not (first and i < 3):
                        mix(u - 3, p if i >= 3 else 1 - p, (i - 3) % HALVES, first and i == 3)
                if not first:
                    positions(g - 1)

            schedule(pe, group)
            U = NG * HALVES
            transpose_probs(U - 2, 2, False)
            mix(U - 3, 1, 5, False)
            transpose_probs(U - 1, 3, False)
            mix(U - 2, 1, 6, False)
            mix(U - 1, 1, 7, False)
            out_heads(NG - 1, 1, 0, HEADS)
            transpose_y(NG - 1)
            transpose_xn(NG - 1, 1)
            route_logits(NG - 1)
            positions(NG - 1)
            pe.wait_ge(slot_done, NG)

            def transpose_weights(e, p, loaded, first):
                pe.wait_ge(in_ew[p], loaded)
                for i in range(3):
                    n = e * 3 + i
                    if not (first and i < 2):
                        pe.wait_ge(ewt_copied, n - 1 if i == 2 else n)
                    for c in range(FC):
                        mm = pe.transpose((tr_bank, r_bank, tr_bank)[i][:, c * P:(c + 1) * P], ew[:, p, i, c],
                                          ident[:])
                    mm.then_inc(ewt_done, 1)

            def transpose_inputs(e, p, loaded, first):
                pe.wait_ge(in_xe[p], loaded)
                pe.wait_ge(ewt_copied, e * 3 + 3 if not first else 6)
                for c in range(SC):
                    b, o = (y_bank, c) if c < 4 else (px_bank, 0)
                    mm = pe.transpose(b[:, o * P:(o + 1) * P], xe[:, p, c], ident[:])
                    if c == 3:
                        mm.then_inc(xet_done, 1)
                mm.then_inc(xet_done, 1)

            transpose_weights(0, 0, 48, True)
            transpose_weights(1, 1, 48, False)

            def expert(e, p, eh, more, first):
                if not first:
                    pe.wait_ge(ye_copied, e * 2)
                transpose_inputs(e, p, eh * 16 + 16, first)
                pe.wait_ge(xet_copied, e * 2 + 2)
                for i in range(2 * FC):
                    f, k = divmod(i, 2)
                    n = e * 2 * FC + i
                    if not (first and i < 2):
                        pe.wait_ge(hid_done, n - 1)
                    rhs = xe_t[:, p, k * CAP:(k + 1) * CAP]
                    pe.matmul(sc_bank[i % 2][:, 0:CAP], ewt[:, p, 0, f], rhs, start=True, stop=True)
                    pe.matmul(q_bank[i % 2][:, 0:CAP], ewt[:, p, 1, f], rhs, start=True, stop=True
                              ).then_inc(gu_done, 1)
                pe.wait_ge(hid_done, (e + 1) * 2 * FC)
                for c in range(SC):
                    b, o = (y_bank, c) if c < 4 else (px_bank, 0)
                    for f in range(FC):
                        mm = pe.matmul(b[:, o * P:(o + 1) * P], hid[:, p, f, c * P:(c + 1) * P], ewt[:, p, 2, f],
                                       start=(f == 0), stop=(f == FC - 1))
                    if c == 3:
                        mm.then_inc(ye_done, 1)
                mm.then_inc(ye_done, 1)
                if more:
                    transpose_weights(e + 2, p, eh * 48 + 96, False)

            expert(0, 0, 0, True, True)
            expert(1, 1, 0, True, False)
            with pe.Fori(1, E // 2 - 1) as it:
                expert(it * 2, 0, it, True, False)
                expert(it * 2 + 1, 1, it, True, False)
            expert(E - 2, 0, E // 2 - 1, False, False)
            expert(E - 1, 1, E // 2 - 1, False, False)

        @block.vector
        def _(dve):
            dve.wait_ge(in_gate, 64)
            dve.tensor_scalar(mask_add[:], mask_u8[:], MASKED, MASKED, ALU.mult, ALU.subtract
                              ).then_inc(small_done, 1)

            def ln_stats(n, p, loads):
                dve.wait_ge(in_raw[p], loads * 32)
                for b in range(GB):
                    dve.bn_stats(stats[:, b], raw[:, p, b]).then_inc(stats_step, 1)
                dve.wait_ge(stats_step, n * 2 * GB + GB)
                apart(dve)
                for b in range(GB):
                    dve.bn_aggr(moments[:, b], stats[:, b]).then_inc(stats_step, 1)

            def ln_normalise(n, p):
                dve.wait_ge(rstd_step, n * 2 + 2)
                for b in range(GB):
                    ins = dve.tensor_scalar(normed[:, p, b], raw[:, p, b], moments[:, b, 0:1], rstd[:, b:b + 1],
                                            ALU.subtract, ALU.mult)
                ins.then_inc(normed_done, 1)

            def copy_xt(n, p):
                dve.wait_ge(xt_done, n + 1)
                dve.tensor_copy(XT[:, p].rearrange("p b k -> p (b k)"), r_bank[:]).then_inc(xt_copied, 1)

            ln_stats(0, 0, 1)
            ln_normalise(0, 0)
            copy_xt(0, 0)
            dve.wait_ge(gate_done, 1)
            dve.tensor_copy(gate_t[:], y_bank[:, 0:E]).then_inc(small_done, 1)
            for k in range(8):
                dve.wait_ge(ab_done, k + 1)
                src = setup_banks[k % 6][:].rearrange("p (h d) -> p h d", h=4)
                h0 = 8 * (k % 4 // 2) + k % 2
                if k < 4:
                    dve.tensor_scalar(A[:, h0:h0 + 7:2], src, SCALE, None, ALU.mult).then_inc(ab_copied, 1)
                else:
                    dve.tensor_copy(Bw[:, h0:h0 + 7:2], src).then_inc(ab_copied, 1)

            def q_copy(n, p, k):
                dve.wait_ge(q_done, n * 8 + k + 1)
                dve.tensor_copy(q[:, p, :, 2 * k:2 * k + 2, :].rearrange("p b h s -> p h b s"),
                                q_bank[k % 2][:].rearrange("p (h b s) -> p h b s", h=2, b=GB)
                                ).then_inc(q_copied_dve, 1)

            for k in range(0, 8, 2):
                q_copy(0, 0, k)

            def row_max(u, i, early):
                dve.wait_ge(s_done, u + 1)
                if not early:
                    dve.wait_ge(norm_done, u - 3)
                dve.tensor_reduce(neg_max[:, i % 4], sc_bank[i % 2][:].rearrange("p (j k) -> p j k", j=PAIRS),
                                  AX_X, ALU.max, negate=True).then_inc(max_done, 1)

            def row_recip(u, i):
                dve.wait_ge(exp_done, (u + 1) * PAIRS)
                dve.reciprocal(rsums[:, i % 4], sums[:, i % 4]).then_inc(recip_done, 1)

            def copy_px(v, p, i):
                dve.wait_ge(px_done, v + 1)
                b, hf = divmod(i, 2)
                dve.tensor_copy(px[:, p, b, 8 * hf:8 * hf + 8].rearrange("p h s -> p (h s)"), px_bank[:]
                                ).then_inc(px_copied, 1)

            def residual(n, p, nh):
                dve.wait_ge(yt_done, n + 1)
                dve.wait_ge(in_resid[p], nh * 16 + 16)
                dve.wait_ge(x1_kept[p], nh + 1)
                dve.scalar_tensor_tensor(x1[:, p].rearrange("p c d -> p (c d)"), r_bank[:, 0:GT], tanhs[:, 0:1],
                                         resid[:, p].rearrange("p c d -> p (c d)"), ALU.mult, ALU.add
                                         ).then_inc(x1_done, 1)
                dve.wait_ge(x1_done, n + 1)
                for c in range(TC):
                    dve.bn_stats(t_stats[:, c], x1[:, p, c]).then_inc(t_stats_step, 1)
                dve.wait_ge(t_stats_step, n * 2 * TC + TC)
                apart(dve)
                for c in range(TC):
                    dve.bn_aggr(t_moments[:, c], t_stats[:, c]).then_inc(t_stats_step, 1)

            def token_norm(n, p):
                dve.wait_ge(t_rstd_step, n * 2 + 2)
                dve.wait_ge(xn_free, n + 1)
                for c in range(TC):
                    dve.tensor_scalar(xn[:, p, c], x1[:, p, c], t_moments[:, c, 0:1], t_rstd[:, c:c + 1],
                                      ALU.subtract, ALU.mult).then_inc(xn_done, 1)

            ROUTE = 6

            def route(n):
                done = [0]

                def step(ins):
                    ins.then_inc(route_step, 1)
                    done[0] += 1
                    dve.wait_ge(route_step, n * ROUTE + done[0])

                dve.wait_ge(logits_done, n + 1)
                step(dve.tensor_copy(logits[:].rearrange("p c e -> p (c e)"), r_bank[:, 0:TC * E]))
                apart(dve)
                for c in range(TC):
                    dve.max(top[:, c], logits[:, c]).then_inc(route_step, 1)
                done[0] += TC
                dve.wait_ge(route_step, n * ROUTE + done[0])
                dve.tensor_tensor(gap[:], top[:, :, 1], top[:, :, 0], ALU.subtract).then_inc(gap_done, 1)
                for c in range(TC):
                    dve.max_index(top_i[:, c], top[:, c], logits[:, c]).then_inc(route_step, 1)
                done[0] += TC
                dve.wait_ge(route_step, n * ROUTE + done[0])
                step(dve.tensor_copy(choice[:].rearrange("p (c k) -> p c k", k=TOP_K), top_i[:, :, 0:TOP_K]))
                dve.wait_ge(counts_step, n * TC + 1)
                dve.tensor_tensor(onehot[:], iota_e[:].unsqueeze(1).broadcast_to((P, TC * TOP_K, E)),
                                  choice[:].unsqueeze(2).broadcast_to((P, TC * TOP_K, E)), ALU.is_equal
                                  ).then_inc(onehot_done, 1)
                assert done[0] == ROUTE

            PLACE = 9

            def place(n, p):
                done = [0]

                def step(ins):
                    ins.then_inc(place_step, 1)
                    done[0] += 1
                    dve.wait_ge(place_step, n * PLACE + done[0])

                dve.wait_ge(ratio_done, n + 1)
                step(dve.tensor_scalar(ratio1[:], ratio[:], 1.0, None, ALU.add))
                step(dve.reciprocal(wts[:, :, 0], ratio1[:]))
                step(dve.tensor_tensor(wts[:, :, 1], ratio[:], wts[:, :, 0], ALU.mult))
                dve.wait_ge(wts_kept, n + 1)
                dve.tensor_scalar(wts_g[:], wts[:], tanhs[:, 1:2], None, ALU.mult).then_inc(wts_done, 1)
                dve.wait_ge(pos_done, n + 1)
                step(dve.tensor_tensor(placed[:], r_bank[:, 64:64 + TC * TOP_K * E].rearrange(
                    "p (c e) -> p c e", e=E), onehot[:], ALU.mult))
                step(dve.tensor_reduce(pos[:], placed[:], AX_X, ALU.add))
                step(dve.scalar_tensor_tensor(base[:], choice[:], float(ROWS), k_offset[:], ALU.mult, ALU.add))
                step(dve.tensor_tensor(base[:], base[:], pos[:], ALU.add))
                step(dve.tensor_scalar(valid[:], pos[:], float(CAP), None, ALU.is_lt))
                step(dve.scalar_tensor_tensor(moved[:], base[:], float(-SLOTS), valid[:], ALU.add, ALU.mult))
                dve.wait_ge(slot_kept, n + 1)
                dve.tensor_scalar(slot[:, p], moved[:], float(SLOTS), None, ALU.add).then_inc(slot_done, 1)
                assert done[0] == PLACE

            dve.wait_ge(tanh_done, 1)
            dve.wait_ge(consts, 1)

            def group(g, p, gh, first, last):
                nh = gh + p
                for i in range(HALVES):
                    u = g * HALVES + i
                    row_max(u, i, first and i < 4)
                    if not last:
                        if i == 0:
                            ln_stats(g + 1, 1 - p, nh + 1)
                        if i == 2:
                            ln_normalise(g + 1, 1 - p)
                        if i == 4:
                            copy_xt(g + 1, 1 - p)
                    row_recip(u, i)
                    if not first:
                        if i == 5:
                            residual(g - 1, 1 - p, gh + p - 1)
                        if i == 6:
                            token_norm(g - 1, 1 - p)
                        if i == 7:
                            route(g - 1)
                    if not last and i >= 5:
                        for k in {5: (0, 2), 6: (4,), 7: (6,)}[i]:
                            q_copy(g + 1, 1 - p, k)
                    if not (first and i < 3):
                        copy_px(u - 3, p if i >= 3 else 1 - p, (i - 3) % HALVES)
                if not first:
                    place(g - 1, 1 - p)

            schedule(dve, group)
            U = NG * HALVES
            for i in range(5, 8):
                copy_px(U - 8 + i, 1, i)
            residual(NG - 1, 1, NG // 2 - 1)
            token_norm(NG - 1, 1)
            route(NG - 1)
            place(NG - 1, 1)

            def copy_inputs(e, p):
                dve.wait_ge(xet_done, e * 2 + 1)
                dve.tensor_copy(xe_t[:, p, 0:512], y_bank[:]).then_inc(xet_copied, 1)
                dve.wait_ge(xet_done, e * 2 + 2)
                dve.tensor_copy(xe_t[:, p, 512:ROWS], px_bank[:, 0:ROWS - 512]).then_inc(xet_copied, 1)

            def expert(e, p, eh):
                copy_inputs(e, p)
                for i in range(2 * FC):
                    f, k = divmod(i, 2)
                    dve.wait_ge(silu_done, e * 2 * FC + i + 1)
                    dve.tensor_tensor(hid[:, p, f, k * CAP:(k + 1) * CAP], silu[:, i % 2],
                                      q_bank[i % 2][:, 0:CAP], ALU.mult).then_inc(hid_done, 1)
                if eh is not None:
                    dve.wait_ge(y_stored[p], eh * 16)
                dve.wait_ge(ye_done, e * 2 + 1)
                dve.tensor_copy(ye[:, p, 0:4].rearrange("p c d -> p (c d)"), y_bank[:]).then_inc(ye_copied, 1)
                dve.wait_ge(ye_done, e * 2 + 2)
                dve.tensor_copy(ye[:, p, 4], px_bank[:, 0:D]).then_inc(ye_copied, 1)

            expert(0, 0, None)
            expert(1, 1, None)
            with dve.Fori(1, E // 2) as it:
                expert(it * 2, 0, it)
                expert(it * 2 + 1, 1, it)

            def combine(c, r, rounds, again):
                dve.wait_ge(picked[r], rounds * 32 + 32)
                if again:
                    dve.wait_ge(stored[r], rounds * 16)
                dve.scalar_tensor_tensor(part[:, r], y_pick[:, r, 0], wts_all[:, bass.ds(c, 1), 0].rearrange("p c -> p c"),
                                         x1_all[:, bass.ds(c, 1), :].rearrange("p c d -> p (c d)"),
                                         ALU.mult, ALU.add).then_inc(part_done, 1)
                dve.wait_ge(part_done, c + 1)
                dve.scalar_tensor_tensor(final[:, r], y_pick[:, r, 1], wts_all[:, bass.ds(c, 1), 1],
                                         part[:, r], ALU.mult, ALU.add).then_inc(final_done, 1)

            for p in range(2):
                dve.wait_ge(x1_kept[p], NG // 2 + 1)
            dve.wait_ge(wts_kept, NG + 1)
            for r in range(4):
                combine(r, r, 0, False)
            with dve.Fori(1, NT // 4) as it:
                for r in range(4):
                    combine(it * 4 + r, r, it, True)


_INS = ['x', 'ctx_1024', 'mask_BxS2_bk0', 'g_xattn', 'g_ffn', 'L0_xattn_g1', 'L0_xattn_b1', 'L0_xattn_g2',
        'L0_xattn_b2', 'L0_xattn_Wq', 'L0_xattn_Wkv', 'L0_xattn_Wout', 'L0_ffn_gate_w', 'L0_ffn_wi_gate',
        'L0_ffn_wi_up', 'L0_ffn_wo']
_OUT = ((32, 64, 128), 'float32')


def kernel(**inputs):
    import numpy as _np
    import concourse.bacc as _bacc
    from concourse import mybir as _mybir
    from concourse.bass_utils import run_bass_kernel_spmd as _run

    nc = _bacc.Bacc("TRN2", target_bir_lowering=False, num_devices=1)
    arrays, args = {}, []
    for name in _INS:
        a = _np.ascontiguousarray(inputs[name])
        arrays[f"in_{name}_dram"] = a
        args.append(nc.dram_tensor(f"in_{name}_dram", a.shape, _mybir.dt.from_np(a.dtype), kind="ExternalInput").ap())
    out = nc.dram_tensor("out_0_dram", _OUT[0], _mybir.dt.from_np(_np.dtype(_OUT[1])), kind="ExternalOutput").ap()
    flamingo_block(nc, *args, out)
    r = _run(nc, [arrays], core_ids=[0])
    return r.results[0]["out_0_dram"]
```

```python
from contextlib import ExitStack

import concourse.bass as bass
from concourse import mybir

F32 = mybir.dt.float32
F32R = mybir.dt.float32r
BF16 = mybir.dt.bfloat16
U32 = mybir.dt.uint32
I32 = mybir.dt.int32
U8 = mybir.dt.uint8
ALU = mybir.AluOpType
ACT = mybir.ActivationFunctionType
AX_X = mybir.AxisListType.X

P = 128
B, S, D = 32, 64, 128
HEADS, DH = 16, 64
EPS = 1e-5
E, F = 8, 512
TOP_K = 2
N = B * S
CAP = max(int(N / E * 1.25), 1)
ROWS = TOP_K * CAP
SLOTS = E * ROWS
SCALE = 1.0 / float(DH) ** 0.5
MASKED = 1e30

GB = 4
NG = B // GB
HALVES = 2 * GB
PAIRS = 4
GT = GB * S
TC = GT // P
ROW = D + 1
EMPTY = float(1 << 22)
FC = F // P
SC = ROWS // P
NT = N // P
HEADS_OF_SLOT = {2: (0, 3), 3: (3, 6), 4: (6, 9), 5: (9, 12), 6: (12, 14), 7: (14, 16)}
assert ROWS % P == 0 and CAP <= 512 and NG % 2 == 0


def flamingo_block(nc, x, ctx_in, mask, g_xattn, g_ffn, g1, b1, g2, b2, Wq, Wkv, Wout,
                   gate_w, wi_gate, wi_up, wo, out):
    with ExitStack() as ctx:
        def sb(name, shape, dt=F32, scope=ctx):
            return scope.enter_context(nc.sbuf_tensor(name, shape, dt))

        def bank(name):
            return ctx.enter_context(nc.psum_tensor(name, [P, 512], F32))

        def sem(name):
            return ctx.enter_context(nc.semaphore(name))

        x_flat = x.rearrange("b s d -> (b s) d")
        out_flat = out.rearrange("b s d -> (b s) d")
        x_slots = nc.dram_tensor("x_slots", (SLOTS, ROW), F32).ap()
        y_tokens = nc.dram_tensor("y_tokens", (TOP_K * N, D), F32).ap()

        x1_tokens = nc.dram_tensor("x1_tokens", (N, D), F32).ap()

        ident = sb("ident", [P, P])
        before = sb("before", [P, P], BF16)
        ones = sb("ones", [P, P], BF16)
        iota_i = sb("iota_i", [P, E], I32)
        iota_e = sb("iota_e", [P, E])
        token_i = sb("token_i", [P, NT], I32)
        token_f = sb("token_f", [P, NT])
        k_offset = sb("k_offset", [P, TC * TOP_K])
        row_offset = sb("row_offset", [P, SC])
        minus_half = sb("minus_half", [P, GB])
        var_scale = sb("var_scale", [P, 1])
        var_eps = sb("var_eps", [P, 1])
        gate_t = sb("gate_t", [P, E])
        affine = sb("affine", [P, 2, D])
        gains = sb("gains", [P, 2])
        tanhs = sb("tanhs", [P, 2])
        A = sb("A", [P, 2, HEADS, D], F32R)
        Bw = sb("Bw", [P, 2, HEADS, D], F32R)
        tok = sb("tok", [P, 2, GB, D])
        X = sb("X", [P, 2, 2, GB, D], F32R)
        XT = sb("XT", [P, 2, 2, GB, P], F32R)
        stats = sb("stats", [P, GB, 6])
        moments = sb("moments", [P, GB, 2])
        var_adj = sb("var_adj", [P, GB])
        rstd = sb("rstd", [P, GB])
        mask_u8 = sb("mask_u8", [1, 2, GT], U8)
        mask_g = sb("mask_g", [1, 2, GB, S], BF16)
        neg_max = sb("neg_max", [P, 2, PAIRS])
        sums = sb("sums", [P, 2, PAIRS])
        rsums = sb("rsums", [P, 2, PAIRS])
        probs = sb("probs", [P, 2, PAIRS, P])
        probs_t = sb("probs_t", [P, 2, 2, 512], F32R)
        yt = sb("yt", [P, TC, P])
        x1 = sb("x1", [P, 2, TC, D])
        t_stats = sb("t_stats", [P, TC, 6])
        t_moments = sb("t_moments", [P, TC, 2])
        t_var = sb("t_var", [P, TC])
        t_rstd = sb("t_rstd", [P, TC])
        xn = sb("xn", [P, 2, TC, ROW])
        xn_t = sb("xn_t", [P, TC, P])
        logits = sb("logits", [P, TC, E])
        top = sb("top", [P, TC, 8])
        top_i = sb("top_i", [P, TC, 8], U32)
        choice = sb("choice", [P, TC * TOP_K])
        onehot = sb("onehot", [P, TC * TOP_K, E], BF16)
        counts = sb("counts", [P, TOP_K * E], BF16)
        placed = sb("placed", [P, TC * TOP_K, E])
        pos = sb("pos", [P, TC * TOP_K])
        base = sb("base", [P, TC * TOP_K])
        base_k = sb("base_k", [P, TC * TOP_K])
        valid = sb("valid", [P, TC * TOP_K])
        moved = sb("moved", [P, TC * TOP_K])
        slot = sb("slot", [P, 2, TC * TOP_K], U32)
        gap = sb("gap", [P, TC])
        ratio = sb("ratio", [P, TC])
        ratio1 = sb("ratio1", [P, TC])
        wts = sb("wts", [P, TC, TOP_K])
        wts_g = sb("wts_g", [P, TC, TOP_K])
        wts_all = sb("wts_all", [P, NT, TOP_K])
        row_i = sb("row_i", [P, 2, SC], U32)

        with ExitStack() as first:
            wq_sb = sb("wq_sb", [P, HEADS * DH], F32, first)
            wkv_sb = sb("wkv_sb", [P, 2 * HEADS * DH], F32, first)
            wout_sb = sb("wout_sb", [P, HEADS // 2, D], F32, first)
            gate_sb = sb("gate_sb", [E, D], F32, first)
            w_t = sb("w_t", [P, 3 * HEADS // 2, P], F32, first)
            empty = sb("empty", [P, SC, ROW], F32, first)
        with ExitStack() as second:
            px = sb("px", [P, 2, 2, GB, HEADS, S], F32R, second)
            q = sb("q", [P, 2, 2, GB, HEADS, S], F32R, second)
        with ExitStack() as third:
            hid = sb("hid", [P, TOP_K, 2, FC, CAP], F32R, third)
            hid_full = sb("hid_full", [P, 4, CAP], F32, third)
            yet = sb("yet", [P, ROWS], F32, third)
            ye = sb("ye", [P, 2, SC, D], F32, third)
            silu = sb("silu", [P, 2, CAP], F32, third)
            xe_t = sb("xe_t", [P, 2, 2, SC * P], F32R, third)
            xe = sb("xe", [P, 2, SC, ROW], F32, third)
            ewt = sb("ewt", [P, 2, 3, 2, FC, P], F32R, third)
            ew = sb("ew", [P, 2, 3, FC, P], F32, third)
            x1_all = sb("x1_all", [P, NT, D], F32, third)
        with ExitStack() as fourth:
            y_pick = sb("y_pick", [P, TOP_K, NT, D], F32, fourth)
            part = sb("part", [P, NT, D], F32, fourth)
            final = sb("final", [P, NT, D], F32, fourth)

        sc_bank = [bank("sc0"), bank("sc1")]
        tr_bank = bank("tr")
        px_bank = bank("pxb")
        q_bank = [bank("q0"), bank("q1")]
        y_bank = bank("yb")
        r_bank = bank("rb")
        setup_banks = [sc_bank[0], sc_bank[1], tr_bank, px_bank, q_bank[0], q_bank[1]]

        in_qkv, in_wout, in_affine, in_small = sem("in_qkv"), sem("in_wout"), sem("in_affine"), sem("in_small")
        in_tok = [sem("in_tok0"), sem("in_tok1")]
        in_resid = [sem("in_resid0"), sem("in_resid1")]
        empty_ready, slots_empty = sem("empty_ready"), sem("slots_empty")
        const_step, consts = sem("const_step"), sem("consts")
        gate_copied, tanh_done = sem("gate_copied"), sem("tanh_done")
        wt_done, wt_copied = sem("wt_done"), sem("wt_copied")
        ab_done, ab_hi, ab_lo = sem("ab_done"), sem("ab_hi"), sem("ab_lo")
        gate_done = sem("gate_done")
        stats_step, rstd_step = sem("stats_step"), sem("rstd_step")
        normed_done, scaled_done, tok_done = sem("normed_done"), sem("scaled_done"), sem("tok_done")
        X_hi, X_lo = sem("X_hi"), sem("X_lo")
        xt_done, xt_hi, xt_lo = sem("xt_done"), sem("xt_hi"), sem("xt_lo")
        q_done, q_hi, q_lo = sem("q_done"), sem("q_hi"), sem("q_lo")
        mask_ready = sem("mask_ready")
        s_done, max_done, exp_done = sem("s_done"), sem("max_done"), sem("exp_done")
        recip_done, norm_done = sem("recip_done"), sem("norm_done")
        tr_done, tr_hi, tr_lo = sem("tr_done"), sem("tr_hi"), sem("tr_lo")
        px_done, px_hi, px_lo = sem("px_done"), sem("px_hi"), sem("px_lo")
        y_done, y_copied, yt_done = sem("y_done"), sem("y_copied"), sem("yt_done")
        x1_done, t_stats_step, t_rstd_step = sem("x1_done"), sem("t_stats_step"), sem("t_rstd_step")
        xn_done, xnt_done, xnt_copied = sem("xn_done"), sem("xnt_done"), sem("xnt_copied")
        logits_done, route_step, place_step = sem("logits_done"), sem("route_step"), sem("place_step")
        gap_done, ratio_done, wts_done = sem("gap_done"), sem("ratio_done"), sem("wts_done")
        onehot_done, pos_done, counts_step = sem("onehot_done"), sem("pos_done"), sem("counts_step")
        slot_done = sem("slot_done")
        x1_stored, in_x1, wts_kept = [sem("x1_stored0"), sem("x1_stored1")], sem("in_x1"), sem("wts_kept")
        scattered, xn_free = [sem("scattered0"), sem("scattered1")], sem("xn_free")
        in_ew = [sem("in_ew0"), sem("in_ew1")]
        in_xe = [sem("in_xe0"), sem("in_xe1")]
        turned, turned_hi, turned_lo, rows_done = sem("turned"), sem("turned_hi"), sem("turned_lo"), sem("rows_done")
        gu_done, silu_done, hid_done = sem("gu_done"), sem("silu_done"), sem("hid_done")
        hid_hi, hid_lo = sem("hid_hi"), [sem("hid_lo_first"), sem("hid_lo_second")]
        yet_done, yet_copied, ye_done, ye_copied, ye_free, y_sent = sem("yet_done"), sem("yet_copied"), sem("ye_done"), sem("ye_copied"), sem("ye_free"), sem("y_sent")
        waits_met = sem("waits_met")
        picked = [sem(f"picked{r}") for r in range(4)]
        part_done, final_done, stored = sem("part_done"), sem("final_done"), sem("stored")

        def apart(eng):
            eng.sem_inc(waits_met, 1)

        def schedule(eng, body):
            body(0, 0, False, False, True, True)
            body(1, 1, True, False, True, True)
            with eng.Fori(1, NG // 2 - 1) as it:
                body(it * 2, 0, True, True, True, True)
                body(it * 2 + 1, 1, True, True, True, True)
            body(NG - 2, 0, True, True, False, True)
            body(NG - 1, 1, True, True, False, False)

        def experts(eng, body):
            body(0, 0, 1)
            body(1, 1, 2)
            with eng.Fori(1, E // 2 - 1) as it:
                body(it * 2, 0, it + 1)
                body(it * 2 + 1, 1, it + 2)
            body(E - 2, 0, E // 2)
            body(E - 1, 1, None)

        TURNS = 5
        TURN_AFTER = {0: 0, 1: 1, 2: 2, 5: 3, 6: 4}
        TURN_BANK = (tr_bank, r_bank, tr_bank, r_bank, tr_bank)
        BACK_BANK = (r_bank, tr_bank)
        Y_BANK = (px_bank, y_bank)
        UNITS = TOP_K * FC

        def flat(ap):
            names = "abcdef"[:ap.ndim - 1]
            return ap.rearrange(f"p {' '.join(names)} -> p ({' '.join(names)})")

        def turned_into(part, p, j):
            if j < 3:
                return flat(ewt[:, p, j, part])
            return xe_t[:, p, part, 0:512] if j == 3 else xe_t[:, p, part, 512:ROWS]

        def turn_bank(e, j):
            if isinstance(e, int) and e == 0:
                return (sc_bank[0], sc_bank[1], q_bank[0], r_bank, tr_bank)[j]
            return TURN_BANK[j]

        LAST = NG * HALVES

        block = ctx.enter_context(nc.Block())

        @block.sync
        def _(sp):
            def load_tok(n, p):
                sp.dma_start(tok[0:S, p], ctx_in[n * GB:(n + 1) * GB].rearrange("b s d -> s b d")).then_inc(in_tok[p], 16)
                sp.dma_start(tok[S:P, p], x[n * GB:(n + 1) * GB].rearrange("b s d -> s b d")).then_inc(in_tok[p], 16)
                sp.dma_start(mask_u8[:, p], mask[n * GB:(n + 1) * GB].rearrange("b s -> (b s)").unsqueeze(0)
                             ).then_inc(in_tok[p], 16)

            def load_resid(n, p):
                sp.dma_start(x1[:, p], x_flat[n * GT:(n + 1) * GT, :].rearrange("(c p) d -> p c d", p=P)
                             ).then_inc(in_resid[p], 16)

            sp.dma_start(wq_sb[:], Wq).then_inc(in_qkv, 16)
            load_tok(0, 0)
            sp.dma_start(wkv_sb[:], Wkv).then_inc(in_qkv, 16)
            sp.dma_start(wout_sb[:], Wout.rearrange("(c p) e -> p c e", p=P)).then_inc(in_wout, 16)
            load_tok(1, 1)
            load_resid(0, 0)
            load_resid(1, 1)
            sp.wait_ge(empty_ready, 2)
            for e in range(E):
                sp.dma_start(x_slots[e * ROWS:(e + 1) * ROWS, :].rearrange("(c p) d -> p c d", p=P),
                             empty[:]).then_inc(slots_empty, 16)
            for c in range(TOP_K * NT // 4):
                sp.dma_start(y_tokens[c * 512:(c + 1) * 512, :].rearrange("(c p) d -> p c d", p=P),
                             empty[:, 0:4, 0:D]).then_inc(slots_empty, 16)

            for n in range(2, 5):
                sp.wait_ge(xt_done, n - 1)
                sp.wait_ge(X_lo, n - 1)
                sp.wait_ge(mask_ready, n - 1)
                load_tok(n, n % 2)
            def store_x1(n, p):
                sp.wait_ge(x1_done, n + 1)
                sp.dma_start(x1_tokens[n * GT:(n + 1) * GT, :].rearrange("(c p) d -> p c d", p=P), x1[:, p]
                             ).then_inc(x1_stored[p], 16)

            for n in range(2, NG):
                p = n % 2
                store_x1(n - 2, p)
                if n + 3 < NG:
                    sp.wait_ge(xt_done, n + 2)
                    sp.wait_ge(X_lo, n + 2)
                    sp.wait_ge(mask_ready, n + 2)
                    load_tok(n + 3, 1 - p)
                sp.wait_ge(x1_stored[p], n // 2 * 16)
                sp.wait_ge(xn_done, (n - 1) * (TC + 1))
                load_resid(n, p)
                sp.wait_ge(scattered[p], n // 2 * 16 * TC * TOP_K)
                sp.sem_inc(xn_free, 1)

            def load_expert(e, p):
                for j, w in enumerate((wi_gate, wi_up)):
                    sp.dma_start(ew[:, p, j], w[bass.ds(e, 1)].rearrange("o (c p) d -> p (o c) d", p=P)
                                 ).then_inc(in_ew[p], 16)
                sp.dma_start(ew[:, p, 2], wo[bass.ds(e, 1)].rearrange("o d (c f) -> d (o c) f", c=FC)
                             ).then_inc(in_ew[p], 16)

            def load_inputs(e, p):
                sp.dma_start(xe[:, p], x_slots[bass.ds(e * ROWS, ROWS), :].rearrange("(c p) d -> p c d", p=P)
                             ).then_inc(in_xe[p], 16)

            sp.wait_ge(s_done, LAST)
            load_expert(0, 0)
            load_expert(1, 1)
            store_x1(NG - 2, 0)
            store_x1(NG - 1, 1)
            for p in range(2):
                sp.wait_ge(scattered[p], 16 * TOP_K * NT // 2)
            load_inputs(0, 0)
            load_inputs(1, 1)
            for p in range(2):
                sp.wait_ge(x1_stored[p], NG // 2 * 16)
            sp.dma_start(x1_all[:], x1_tokens.rearrange("(c p) d -> p c d", p=P)).then_inc(in_x1, 16)

            def next_expert(e, p):
                sp.wait_ge(turned, e * TURNS + TURNS)
                load_expert(e + 2, p)
                sp.wait_ge(rows_done, e + 1)
                load_inputs(e + 2, p)

            with sp.Fori(0, E // 2 - 1) as it:
                next_expert(it * 2, 0)
                next_expert(it * 2 + 1, 1)

            sp.wait_ge(y_sent, 16 * SC * E)
            for r in range(4):
                for k in range(TOP_K):
                    row = k * N + r * 512
                    sp.dma_start(y_pick[:, k, 4 * r:4 * r + 4], y_tokens[row:row + 512, :].rearrange(
                        "(c p) d -> p c d", p=P)).then_inc(picked[r], 16)
            for r in range(4):
                sp.wait_ge(final_done, 4 * r + 4)
                sp.dma_start(out_flat[r * 512:(r + 1) * 512, :].rearrange("(c p) d -> p c d", p=P),
                             final[:, 4 * r:4 * r + 4]).then_inc(stored, 16)
            sp.wait_ge(stored, 64)

        @block.gpsimd
        def _(pool):
            count = [0]

            def const(ins):
                ins.then_inc(const_step, 1)
                count[0] += 1

            for s in (wts_kept, counts_step, y_copied):
                pool.sem_inc(s, 1)
            pool.sem_inc(xn_free, 2)
            const(pool.memset(ident[:], 0.0))
            const(pool.memset(before[:], 0.0))
            pool.wait_ge(const_step, 2)
            const(pool.affine_select(out=ident[:], in_=ident[:], compare_op=ALU.not_equal, fill=1.0, base=0,
                                     pattern=[[-1, P]], channel_multiplier=1))
            const(pool.affine_select(out=before[:], in_=before[:], compare_op=ALU.is_ge, fill=1.0, base=0,
                                     pattern=[[-1, P]], channel_multiplier=1))
            for j, g in enumerate((g1, b1)):
                pool.dma_start(affine[0:S, j], g.partition_broadcast(S)).then_inc(in_affine, 16)
            for j, g in enumerate((g2, b2)):
                pool.dma_start(affine[S:P, j], g.partition_broadcast(S)).then_inc(in_affine, 16)
            const(pool.memset(ones[:], 1.0))
            const(pool.memset(counts[:], 0.0))
            const(pool.memset(minus_half[:], -0.5))
            const(pool.iota(iota_i[:], [[1, E]], base=0, channel_multiplier=0))
            const(pool.iota(token_i[:], [[P, NT]], base=0, channel_multiplier=1))
            for k in range(TC * TOP_K):
                const(pool.memset(k_offset[:, k:k + 1], float(k % TOP_K * CAP)))
            const(pool.memset(row_offset[:], 0.0))
            const(pool.memset(var_scale[:], 1.0))
            const(pool.memset(var_eps[:], EPS))
            pool.wait_ge(const_step, count[0])
            const(pool.memset(var_scale[S:P], 1.0 + EPS))
            const(pool.memset(var_eps[S:P], EPS * EPS))
            pool.wait_ge(const_step, count[0])
            const(pool.affine_select(out=row_offset[:], in_=row_offset[:], compare_op=ALU.is_gt, fill=float(N),
                                     base=CAP, pattern=[[-P, SC]], channel_multiplier=-1))
            pool.wait_ge(const_step, count[0])
            const(pool.tensor_copy(token_f[:], token_i[:]))
            const(pool.tensor_copy(iota_e[:], iota_i[:]))
            pool.wait_ge(const_step, count[0])
            pool.sem_inc(consts, 1)

            def ln_rstd(n):
                pool.wait_ge(stats_step, n * 2 * GB + 2 * GB)
                apart(pool)
                pool.tensor_scalar(var_adj[:], moments[:, :, 1], var_scale[:, 0:1], var_eps[:, 0:1],
                                   ALU.mult, ALU.add).then_inc(rstd_step, 1)
                pool.wait_ge(rstd_step, n * 2 + 1)
                pool.tensor_tensor(rstd[:], var_adj[:], minus_half[:], ALU.pow).then_inc(rstd_step, 1)

            def ln_gain(n, p):
                pool.wait_ge(normed_done, n + 1)
                pool.tensor_tensor(tok[:, p], tok[:, p], affine[:, 0:1, :].broadcast_to((P, GB, D)),
                                   ALU.mult).then_inc(scaled_done, 1)

            def ln_shift(n, p):
                pool.wait_ge(scaled_done, n + 1)
                pool.tensor_tensor(tok[:, p], tok[:, p], affine[:, 1:2, :].broadcast_to((P, GB, D)),
                                   ALU.add).then_inc(tok_done, 1)

            def split_tok(n, p):
                pool.wait_ge(X_hi, n + 1)
                pool.tensor_tensor(X[:, p, 1], tok[:, p], X[:, p, 0].bitcast(F32), ALU.subtract).then_inc(X_lo, 1)

            ln_rstd(0)
            pool.wait_ge(in_affine, 4 * 16)
            ln_gain(0, 0)
            ln_shift(0, 0)
            ln_rstd(1)
            ln_gain(1, 1)
            ln_shift(1, 1)
            split_tok(0, 0)
            pool.memset(empty[:], 0.0).then_inc(empty_ready, 1)
            pool.wait_ge(empty_ready, 1)
            pool.memset(empty[:, :, D:ROW], EMPTY).then_inc(empty_ready, 1)

            def normalise(u, i):
                pool.wait_ge(recip_done, u + 1)
                pool.tensor_tensor(probs[:, i % 2], probs[:, i % 2],
                                   rsums[:, i % 2].unsqueeze(2).broadcast_to((P, PAIRS, P)), ALU.mult
                                   ).then_inc(norm_done, 1)

            def token_rstd(n):
                pool.wait_ge(t_stats_step, n * 2 * TC + 2 * TC)
                apart(pool)
                pool.tensor_scalar(t_var[:], t_moments[:, :, 1], EPS, None, ALU.add).then_inc(t_rstd_step, 1)
                pool.wait_ge(t_rstd_step, n * 2 + 1)
                pool.tensor_tensor(t_rstd[:], t_var[:], minus_half[:, 0:TC], ALU.pow).then_inc(t_rstd_step, 1)

            def number_tokens(n, p):
                pool.wait_ge(xn_free, n + 1)
                apart(pool)
                pool.tensor_copy(xn[:, p, :, D], token_f[:, bass.ds(n * TC, TC)]).then_inc(xn_done, 1)

            def count_tokens(n):
                pool.wait_ge(pos_done, n + 1)
                for c in range(TC):
                    pool.tensor_tensor(counts[:], counts[:], onehot[:, TOP_K * c:TOP_K * (c + 1), :].rearrange(
                        "p k e -> p (k e)"), ALU.add).then_inc(counts_step, 1)
                    pool.wait_ge(counts_step, n * TC + c + 2)
                pool.wait_ge(wts_done, n + 1)
                apart(pool)
                pool.tensor_copy(wts_all[:, bass.ds(n * TC, TC), :], wts_g[:]).then_inc(wts_kept, 1)

            def scatter(n, p, k):
                if k == 0:
                    pool.wait_ge(slot_done, n + 1)
                    apart(pool)
                for c in range(TC):
                    i = TOP_K * c + k
                    pool.indirect_dma_start(x_slots, bass.IndirectOffsetOnAxis(slot[:, p, i:i + 1], 0),
                                            xn[:, p, c], None, bounds_check=SLOTS - 1, oob_is_err=False
                                            ).then_inc(scattered[p], 16)

            pool.wait_ge(slots_empty, 16 * (E + TOP_K * NT // 4))

            def group(g, p, y, tail, ln, more):
                for i in range(HALVES):
                    normalise(g * HALVES + i, i)
                    if tail and i == 0:
                        token_rstd(g - 2)
                        number_tokens(g - 2, p)
                    if ln and i == 1:
                        ln_rstd(g + 2)
                    if more and i == 2:
                        split_tok(g + 1, 1 - p)
                    if ln and i == 3:
                        ln_gain(g + 2, p)
                    if ln and i == 4:
                        ln_shift(g + 2, p)
                    if tail and i == 5:
                        count_tokens(g - 2)
                    if tail and i == 6:
                        scatter(g - 2, p, 0)
                    if tail and i == 7:
                        scatter(g - 2, p, 1)

            schedule(pool, group)
            for n in (NG - 2, NG - 1):
                token_rstd(n)
                number_tokens(n, n % 2)
                count_tokens(n)
                scatter(n, n % 2, 0)
                scatter(n, n % 2, 1)

            def hidden_rest(e, f):
                pool.wait_ge(hid_hi, e * UNITS + f + 1)
                pool.tensor_tensor(hid[:, 0, 1, f], hid_full[:, f], hid[:, 0, 0, f].bitcast(F32),
                                   ALU.subtract).then_inc(hid_lo[0], 1)

            def send_rows(e, p, c):
                pool.indirect_dma_start(y_tokens, bass.IndirectOffsetOnAxis(row_i[:, p, c:c + 1], 0),
                                        ye[:, p, c], None, bounds_check=TOP_K * N - 1, oob_is_err=False
                                        ).then_inc(y_sent, 16)

            def rows_copied(e):
                pool.wait_ge(rows_done, e + 1)
                pool.wait_ge(ye_copied, e * 2 + 2)
                apart(pool)

            def expert(e, p, number):
                first = isinstance(e, int) and e == 0
                if not first:
                    if not (isinstance(e, int) and e == 1):
                        pool.wait_ge(y_sent, (e - 1) * 16 * SC)
                    pool.sem_inc(ye_free, 1)
                for f in range(FC):
                    hidden_rest(e, f)
                if not first:
                    rows_copied(e - 1)
                    for c in range(SC):
                        send_rows(e - 1, 1 - p, c)

            experts(pool, expert)
            pool.wait_ge(y_sent, (E - 1) * 16 * SC)
            rows_copied(E - 1)
            for c in range(SC):
                send_rows(E - 1, 1, c)

        @block.scalar
        def _(act):
            act.dma_start(gains[:, 0:1], g_xattn.partition_broadcast(P)).then_inc(in_small, 16)
            act.dma_start(gains[:, 1:2], g_ffn.partition_broadcast(P)).then_inc(in_small, 16)
            act.dma_start(gate_sb[:], gate_w).then_inc(in_small, 16)
            act.wait_ge(in_small, 48)
            act.activation(tanhs[:], gains[:], ACT.Tanh).then_inc(tanh_done, 1)
            for k in range(6):
                act.wait_ge(wt_done, k + 1)
                act.copy(flat(w_t[:, 4 * k:4 * k + 4]), setup_banks[k][:]).then_inc(wt_copied, 1)

            def xt_round(n, p, src):
                act.wait_ge(xt_done, n + 1)
                act.copy(flat(XT[:, p, 0]), src[:]).then_inc(xt_hi, 1)

            def X_round(n, p):
                if not (isinstance(n, int) and n < 2):
                    act.wait_ge(px_done, (n - 1) * HALVES)
                act.wait_ge(tok_done, n + 1)
                act.copy(X[:, p, 0], tok[:, p]).then_inc(X_hi, 1)

            X_round(0, 0)
            xt_round(0, 0, r_bank)

            def ab_round(k):
                act.wait_ge(ab_done, k + 1)
                h0 = 8 * (k % 4 // 2) + k % 2
                dst = (A if k < 4 else Bw)[:, 0, h0:h0 + 7:2]
                act.activation(dst, setup_banks[k % 6][:].rearrange("p (h d) -> p h d", h=4), ACT.Copy,
                               scale=SCALE if k < 4 else 1.0).then_inc(ab_hi, 1)

            for k in range(8):
                ab_round(k)
            xt_round(1, 1, y_bank)

            def q_round(n, p, k):
                act.wait_ge(q_done, n * 8 + k + 1)
                act.copy(q[:, p, 0, :, 2 * k:2 * k + 2, :].rearrange("p b h s -> p h b s"),
                         q_bank[k % 2][:].rearrange("p (h b s) -> p h b s", h=2, b=GB)).then_inc(q_hi, 1)

            for k in range(8):
                q_round(0, 0, k)

            def softmax(u, i, early):
                r = i % 2
                act.wait_ge(max_done, u + 1)
                if not early:
                    act.wait_ge(tr_done, u - 1)
                for j in range(PAIRS):
                    act.activation(probs[:, r, j], sc_bank[r][:, j * P:(j + 1) * P], ACT.Exp,
                                   bias=neg_max[:, r, j:j + 1], accum_out=sums[:, r, j:j + 1]
                                   ).then_inc(exp_done, 1)

            def probs_round(v, i, early):
                act.wait_ge(tr_done, v + 1)
                if not early:
                    act.wait_ge(px_done, v - 1)
                act.copy(probs_t[:, i % 2, 0], tr_bank[:]).then_inc(tr_hi, 1)

            def px_round(v, p, i):
                b, hf = divmod(i, 2)
                act.wait_ge(px_done, v + 1)
                act.copy(flat(px[:, p, 0, b, 8 * hf:8 * hf + 8]), px_bank[:]).then_inc(px_hi, 1)

            def copy_y(n):
                act.wait_ge(y_done, n + 1)
                act.copy(flat(yt[:]), y_bank[:, 0:GT]).then_inc(y_copied, 1)

            def copy_xnt(n):
                act.wait_ge(xnt_done, n + 1)
                act.copy(flat(xn_t[:]), r_bank[:, 0:GT]).then_inc(xnt_copied, 1)

            def gate_ratio(n):
                act.wait_ge(gap_done, n + 1)
                act.activation(ratio[:], gap[:], ACT.Exp).then_inc(ratio_done, 1)

            act.wait_ge(slots_empty, 16 * (E + TOP_K * NT // 4))

            def group(g, p, y, tail, ln, more):
                start = isinstance(g, int) and g == 0
                for i in range(HALVES):
                    u = g * HALVES + i
                    softmax(u, i, start and i < 2)
                    if ln and i == 7:
                        xt_round(g + 2, p, r_bank)
                    if more:
                        q_round(g + 1, 1 - p, i)
                    if more and i == 1:
                        X_round(g + 1, 1 - p)
                    if not (start and i < 2):
                        px_round(u - 2, p if i >= 2 else 1 - p, (i - 2) % HALVES)
                    if not (start and i < 1):
                        probs_round(u - 1, (i - 1) % 2, start and i < 3)
                    if tail and i == 2:
                        copy_xnt(g - 2)
                    if tail and i == 4:
                        gate_ratio(g - 2)
                    if y and i == 7:
                        copy_y(g - 1)

            schedule(act, group)
            px_round(LAST - 2, 1, HALVES - 2)
            probs_round(LAST - 1, 1, False)
            px_round(LAST - 1, 1, HALVES - 1)

            def turn_round(e, p, j):
                act.wait_ge(turned, e * TURNS + j + 1)
                dst = turned_into(0, p, j)
                act.copy(dst, turn_bank(e, j)[:, 0:dst.shape[1]]).then_inc(turned_hi, 1)

            copy_xnt(NG - 2)
            gate_ratio(NG - 2)
            copy_y(NG - 1)
            for j in range(3):
                turn_round(0, 0, j)
            copy_xnt(NG - 1)
            gate_ratio(NG - 1)
            turn_round(0, 0, 3)
            turn_round(0, 0, 4)

            def hid_round(e, u):
                k, f = divmod(u, FC)
                act.wait_ge(hid_done, e * UNITS + u + 1)
                act.copy(hid[:, k, 0, f], hid_full[:, u % 4]).then_inc(hid_hi, 1)

            def copy_yet(e, k):
                act.wait_ge(yet_done, e * TOP_K + k + 1)
                act.copy(yet[:, k * CAP:(k + 1) * CAP], Y_BANK[k][:, 0:CAP]).then_inc(yet_copied, 1)

            def expert(e, p, number):
                first = isinstance(e, int) and e == 0
                for u in range(UNITS):
                    act.wait_ge(gu_done, e * UNITS + u + 1)
                    act.activation(silu[:, u % 2], sc_bank[u % 2][:, 0:CAP], ACT.Silu).then_inc(silu_done, 1)
                    if not (first and u == 0):
                        if u == 0:
                            hid_round(e - 1, UNITS - 1)
                        else:
                            hid_round(e, u - 1)
                    if u == 2 and not first:
                        copy_yet(e - 1, 1)
                    if u == 6:
                        copy_yet(e, 0)
                    if number is not None and u in TURN_AFTER:
                        turn_round(e + 1, 1 - p, TURN_AFTER[u])

            experts(act, expert)
            hid_round(E - 1, UNITS - 1)
            copy_yet(E - 1, 1)

        @block.tensor
        def _(pe):
            def product(o, w, v, n, start=True, stop=True, **kw):
                for t, (a, b) in enumerate(((0, 0), (0, 1), (1, 0))):
                    mm = pe.matmul(o, w(a), v(b), start=start and t == 0, stop=stop and t == 2, **kw)
                return mm

            pe.wait_ge(consts, 1)
            pe.wait_ge(in_qkv, 32)
            for k in range(6):
                for j in range(4):
                    c = 4 * k + j
                    src = wq_sb[:, c * P:(c + 1) * P] if c < 8 else wkv_sb[:, (c - 8) * P:(c - 7) * P]
                    mm = pe.transpose(setup_banks[k][:, j * P:(j + 1) * P], src, ident[:])
                mm.then_inc(wt_done, 1)

            def transpose_tok(n, p, dst):
                pe.wait_ge(tok_done, n + 1)
                for b in range(GB):
                    mm = pe.transpose(dst[:, b * P:(b + 1) * P], tok[:, p, b], ident[:])
                mm.then_inc(xt_done, 1)

            transpose_tok(0, 0, r_bank)
            pe.wait_ge(in_small, 48)
            pe.transpose(y_bank[:, 0:E], gate_sb[:], ident[0:E, 0:E]).then_inc(gate_done, 1)
            pe.wait_ge(in_wout, 16)
            pe.wait_ge(wt_copied, 6)
            for k in range(8):
                if k >= 6:
                    pe.wait_ge(ab_lo, k - 5)
                for j in range(4):
                    h = 8 * (k % 4 // 2) + 2 * j + k % 2
                    rows = slice(DH * (h % 2), DH * (h % 2) + DH)
                    if k < 4:
                        lhs, rhs = w_t[rows, h // 2], w_t[rows, 8 + h // 2]
                    else:
                        lhs, rhs = w_t[rows, 16 + h // 2], wout_sb[rows, h // 2]
                    mm = pe.matmul(setup_banks[k % 6][:, j * P:(j + 1) * P], lhs, rhs, start=True, stop=True)
                mm.then_inc(ab_done, 1)

            def project(n, p, k, fresh=False):
                if not fresh:
                    pe.wait_ge(q_lo, n * 8 + k - 1)
                for h in (2 * k, 2 * k + 1):
                    mm = product(q_bank[k % 2][:, (h % 2) * GT:(h % 2 + 1) * GT], lambda a: A[:, a, h],
                                 lambda b: XT[:, p, b, :, S:P], GT)
                mm.then_inc(q_done, 1)

            pe.wait_ge(gate_copied, 1)
            transpose_tok(1, 1, y_bank)
            pe.wait_ge(ab_lo, 8)
            pe.wait_ge(xt_lo, 1)
            for k in range(8):
                project(0, 0, k, fresh=k < 2)

            def scores(g, p, u, i, early):
                b, hf = divmod(i, 2)
                if i == 0:
                    pe.wait_ge(mask_ready, g + 1)
                if i < 2:
                    pe.wait_ge(q_lo, g * 8 + 4 * i + 4)
                if not early:
                    pe.wait_ge(exp_done, (u - 1) * PAIRS)
                s = sc_bank[i % 2][:].rearrange("p (j k) -> p j k", j=PAIRS)
                pe.matmul(s[:, :, 0:S], ones[0:1, :], mask_g[:, p, b:b + 1].broadcast_to((1, PAIRS, S)),
                          start=True, stop=False, skip_group_check=True)
                for j in range(PAIRS):
                    h = 2 * (PAIRS * hf + j)
                    mm = product(s[:, j], lambda a: flat(q[:, p, a, b, h:h + 2]), lambda c: XT[:, p, c, b], P,
                                 start=False, stop=j == PAIRS - 1, skip_group_check=True)
                mm.then_inc(s_done, 1)

            def transpose_probs(v, i, early):
                pe.wait_ge(norm_done, v + 1)
                if not early:
                    pe.wait_ge(tr_lo, v)
                for j in range(PAIRS):
                    mm = pe.transpose(tr_bank[:, j * P:(j + 1) * P], probs[:, i % 2, j], ident[:])
                mm.then_inc(tr_done, 1)

            def mix(v, p, i, early):
                pe.wait_ge(tr_lo, v + 1)
                if i == 0:
                    pe.wait_ge(X_lo, 1 if early else mix_group[0] + 1)
                if not early:
                    pe.wait_ge(px_lo, v)
                product(px_bank[:], lambda a: X[:, p, a, i // 2], lambda b: probs_t[:, i % 2, b], 512
                        ).then_inc(px_done, 1)

            mix_group = [0]

            def out_heads(n, p, h0, h1):
                if h0 == 0:
                    pe.wait_ge(px_lo, n * HALVES + HALVES)
                    pe.wait_ge(y_copied, n + 1)
                for h in range(h0, h1):
                    mm = product(y_bank[:, 0:GT], lambda a: Bw[:, a, h], lambda b: px[:, p, b, :, h], GT,
                                 start=h == 0, stop=h == HEADS - 1)
                if h1 == HEADS:
                    mm.then_inc(y_done, 1)

            def transpose_y(n):
                pe.wait_ge(y_copied, n + 2)
                for c in range(TC):
                    mm = pe.transpose(r_bank[:, c * P:(c + 1) * P], yt[:, c], ident[:])
                mm.then_inc(yt_done, 1)

            def transpose_xn(n, p):
                pe.wait_ge(xn_done, n * (TC + 1) + TC + 1)
                for c in range(TC):
                    mm = pe.transpose(r_bank[:, c * P:(c + 1) * P], xn[:, p, c, 0:D], ident[:])
                mm.then_inc(xnt_done, 1)

            def route_logits(n):
                pe.wait_ge(xnt_copied, n + 1)
                for c in range(TC):
                    mm = pe.matmul(r_bank[:, c * E:(c + 1) * E], xn_t[:, c], gate_t[:], start=True, stop=True)
                mm.then_inc(logits_done, 1)

            def positions(n):
                pe.wait_ge(onehot_done, n + 1)
                pe.wait_ge(counts_step, n * TC + 1)
                for c in range(TC):
                    o = r_bank[:, 64 + c * TOP_K * E:64 + (c + 1) * TOP_K * E]
                    hot = [flat(onehot[:, TOP_K * a:TOP_K * (a + 1)]) for a in range(c + 1)]
                    pe.matmul(o, before[:], hot[c], start=True, stop=False)
                    for a in range(c):
                        pe.matmul(o, ones[:], hot[a], start=False, stop=False)
                    mm = pe.matmul(o, ones[:], counts[:], start=False, stop=True)
                mm.then_inc(pos_done, 1)

            def group(g, p, y, tail, ln, more):
                start = isinstance(g, int) and g == 0
                for i in range(HALVES):
                    u = g * HALVES + i
                    mix_group[0] = g
                    scores(g, p, u, i, start and i < 2)
                    if ln and i == 7:
                        if tail:
                            pe.wait_ge(slot_done, g - 1)
                        transpose_tok(g + 2, p, r_bank)
                    if more:
                        if i == 0:
                            pe.wait_ge(xt_lo, g + 2)
                        project(g + 1, 1 - p, i)
                    if tail and i == 0:
                        if isinstance(g, int) and g == NG - 1:
                            pass
                        transpose_y(g - 2)
                    if tail and i == 2:
                        transpose_xn(g - 2, p)
                    if tail and i == 3:
                        route_logits(g - 2)
                    if tail and i == 5:
                        positions(g - 2)
                    if y and i >= 2:
                        out_heads(g - 1, 1 - p, *HEADS_OF_SLOT[i])
                    if not (start and i < 2):
                        mix(u - 2, p if i >= 2 else 1 - p, (i - 2) % HALVES, start and i == 2)
                    if not (start and i < 1):
                        transpose_probs(u - 1, i - 1, start and i == 1)

            schedule(pe, group)
            transpose_y(NG - 2)
            mix(LAST - 2, 1, HALVES - 2, False)
            transpose_probs(LAST - 1, 1, False)
            transpose_xn(NG - 2, 0)
            mix(LAST - 1, 1, HALVES - 1, False)
            route_logits(NG - 2)
            out_heads(NG - 1, 1, 0, HEADS)
            positions(NG - 2)

            def turn(e, p, j, number):
                if not (isinstance(e, int) and e == 0):
                    if j < 3:
                        pe.wait_ge(turned_lo, e * TURNS + max(j - 1, 0))
                    elif not (isinstance(e, int) and e == 1):
                        pe.wait_ge(ye_copied, (e - 2) * 2 + j - 2)
                    else:
                        pe.wait_ge(turned_lo, e * TURNS + j - 1)
                if j == 0:
                    pe.wait_ge(in_ew[p], number * 48)
                if j == 3:
                    pe.wait_ge(in_xe[p], number * 16)
                chunks = (ew[:, p, j, c] for c in range(FC)) if j < 3 else (
                    xe[:, p, c, 0:D] for c in range((j - 3) * 4, min(SC, (j - 2) * 4)))
                for c, chunk in enumerate(chunks):
                    mm = pe.transpose(turn_bank(e, j)[:, c * P:(c + 1) * P], chunk, ident[:])
                mm.then_inc(turned, 1)

            turn(0, 0, 0, 1)
            pe.wait_ge(slot_done, NG - 1)
            transpose_y(NG - 1)
            turn(0, 0, 1, 1)
            transpose_xn(NG - 1, 1)
            turn(0, 0, 2, 1)
            route_logits(NG - 1)
            positions(NG - 1)
            pe.wait_ge(slot_done, NG)
            turn(0, 0, 3, 1)
            turn(0, 0, 4, 1)

            def gate_up(e, p, u):
                k, f = divmod(u, FC)
                if not (isinstance(e, int) and e == 0 and u < 2):
                    pe.wait_ge(hid_done, e * UNITS + u - 1)
                for j, b in enumerate((sc_bank[u % 2], q_bank[u % 2])):
                    mm = product(b[:, 0:CAP], lambda a: ewt[:, p, j, a, f],
                                 lambda c: xe_t[:, p, c, k * CAP:(k + 1) * CAP], CAP)
                mm.then_inc(gu_done, 1)

            def down(e, p, k, f):
                pe.wait_ge(hid_lo[k], e * FC + f + 1)
                if f == 0 and not (isinstance(e, int) and e == 0):
                    pe.wait_ge(yet_copied, e * TOP_K + k - 1)
                mm = product(Y_BANK[k][:, 0:CAP], lambda a: ewt[:, p, 2, a, f], lambda b: hid[:, k, b, f], CAP,
                             start=f == 0, stop=f == FC - 1)
                if f == FC - 1:
                    mm.then_inc(yet_done, 1)

            def turn_back(e, piece, last=False):
                if piece == 0:
                    pe.wait_ge(yet_copied, e * TOP_K + 2)
                if not last:
                    pe.wait_ge(turned_lo, (e + 2) * TURNS + 2 + piece)
                for c in range(4 * piece, min(SC, 4 * piece + 4)):
                    mm = pe.transpose(BACK_BANK[piece][:, c % 4 * P:(c % 4 + 1) * P], yet[:, c * P:(c + 1) * P],
                                      ident[:])
                mm.then_inc(ye_done, 1)

            def expert(e, p, number):
                first = isinstance(e, int) and e == 0
                pe.wait_ge(turned_lo, e * TURNS + TURNS)
                for u in range(UNITS):
                    gate_up(e, p, u)
                    if u >= 2:
                        down(e, p, (u - 2) // FC, (u - 2) % FC)
                    elif not first:
                        down(e - 1, 1 - p, 1, FC - 2 + u)
                    if number is not None and u in TURN_AFTER:
                        turn(e + 1, 1 - p, TURN_AFTER[u], number)
                    if u in (3, 4) and not first:
                        turn_back(e - 1, u - 3, last=number is None)

            experts(pe, expert)
            down(E - 1, 1, 1, FC - 2)
            down(E - 1, 1, 1, FC - 1)
            turn_back(E - 1, 0, last=True)
            turn_back(E - 1, 1, last=True)

        @block.vector
        def _(dve):
            def ln_stats(n, p, loads):
                dve.wait_ge(in_tok[p], loads * 48)
                for b in range(GB):
                    dve.bn_stats(stats[:, b], tok[:, p, b]).then_inc(stats_step, 1)
                dve.wait_ge(stats_step, n * 2 * GB + GB)
                if not isinstance(n, int):
                    apart(dve)
                for b in range(GB):
                    dve.bn_aggr(moments[:, b], stats[:, b]).then_inc(stats_step, 1)

            def ln_normalise(n, p):
                dve.wait_ge(rstd_step, n * 2 + 2)
                for b in range(GB):
                    ins = dve.tensor_scalar(tok[:, p, b], tok[:, p, b], moments[:, b, 0:1], rstd[:, b:b + 1],
                                            ALU.subtract, ALU.mult)
                ins.then_inc(normed_done, 1)

            def rest(out_lo, full, hi, wait_for, value, done, scale=None):
                dve.wait_ge(wait_for, value)
                if scale is None:
                    dve.tensor_tensor(out_lo, full, hi.bitcast(F32), ALU.subtract).then_inc(done, 1)
                else:
                    dve.scalar_tensor_tensor(out_lo, full, scale, hi.bitcast(F32), ALU.mult, ALU.subtract
                                             ).then_inc(done, 1)

            def xt_rest(n, p, src):
                rest(flat(XT[:, p, 1]), src[:], flat(XT[:, p, 0]), xt_hi, n + 1, xt_lo)

            def group_mask(n, p):
                dve.tensor_scalar(mask_g[:, p].rearrange("a b s -> a (b s)"), mask_u8[:, p], MASKED, MASKED,
                                  ALU.mult, ALU.subtract).then_inc(mask_ready, 1)

            ln_stats(0, 0, 1)
            ln_normalise(0, 0)
            group_mask(0, 0)
            ln_stats(1, 1, 1)
            ln_normalise(1, 1)
            dve.wait_ge(gate_done, 1)
            dve.tensor_copy(gate_t[:], y_bank[:, 0:E]).then_inc(gate_copied, 1)
            xt_rest(0, 0, r_bank)
            for k in range(8):
                dst = A if k < 4 else Bw
                h0 = 8 * (k % 4 // 2) + k % 2
                rest(dst[:, 1, h0:h0 + 7:2], setup_banks[k % 6][:].rearrange("p (h d) -> p h d", h=4),
                     dst[:, 0, h0:h0 + 7:2], ab_hi, k + 1, ab_lo, SCALE if k < 4 else None)
            xt_rest(1, 1, y_bank)

            def q_rest(n, p, k):
                dve.wait_ge(q_hi, n * 8 + k + 1)
                for h in (2 * k, 2 * k + 1):
                    ins = dve.tensor_tensor(q[:, p, 1, :, h, :],
                                            q_bank[k % 2][:, (h % 2) * GT:(h % 2 + 1) * GT].rearrange(
                                                "p (b s) -> p b s", b=GB),
                                            q[:, p, 0, :, h, :].bitcast(F32), ALU.subtract)
                ins.then_inc(q_lo, 1)

            for k in range(8):
                q_rest(0, 0, k)

            def row_max(u, i, early):
                dve.wait_ge(s_done, u + 1)
                if not early:
                    dve.wait_ge(norm_done, u - 1)
                dve.tensor_reduce(neg_max[:, i % 2], sc_bank[i % 2][:].rearrange("p (j k) -> p j k", j=PAIRS),
                                  AX_X, ALU.max, negate=True).then_inc(max_done, 1)

            def row_recip(u, i):
                dve.wait_ge(exp_done, (u + 1) * PAIRS)
                dve.reciprocal(rsums[:, i % 2], sums[:, i % 2]).then_inc(recip_done, 1)

            def px_rest(v, p, i):
                b, hf = divmod(i, 2)
                rest(flat(px[:, p, 1, b, 8 * hf:8 * hf + 8]), px_bank[:], flat(px[:, p, 0, b, 8 * hf:8 * hf + 8]),
                     px_hi, v + 1, px_lo)

            def probs_rest(v, i):
                rest(probs_t[:, i % 2, 1], tr_bank[:], probs_t[:, i % 2, 0], tr_hi, v + 1, tr_lo)

            def residual(n, p, nh):
                dve.wait_ge(yt_done, n + 1)
                dve.wait_ge(in_resid[p], nh * 16 + 16)
                dve.scalar_tensor_tensor(flat(x1[:, p]), r_bank[:, 0:GT], tanhs[:, 0:1], flat(x1[:, p]),
                                         ALU.mult, ALU.add).then_inc(x1_done, 1)
                dve.wait_ge(x1_done, n + 1)
                for c in range(TC):
                    dve.bn_stats(t_stats[:, c], x1[:, p, c]).then_inc(t_stats_step, 1)
                dve.wait_ge(t_stats_step, n * 2 * TC + TC)
                apart(dve)
                for c in range(TC):
                    dve.bn_aggr(t_moments[:, c], t_stats[:, c]).then_inc(t_stats_step, 1)

            def token_norm(n, p):
                dve.wait_ge(t_rstd_step, n * 2 + 2)
                dve.wait_ge(xn_free, n + 1)
                for c in range(TC):
                    dve.tensor_scalar(xn[:, p, c, 0:D], x1[:, p, c], t_moments[:, c, 0:1], t_rstd[:, c:c + 1],
                                      ALU.subtract, ALU.mult).then_inc(xn_done, 1)

            ROUTE = 6

            def route(n):
                done = [0]

                def step(*several):
                    for ins in several:
                        ins.then_inc(route_step, 1)
                        done[0] += 1
                    dve.wait_ge(route_step, n * ROUTE + done[0])

                dve.wait_ge(logits_done, n + 1)
                step(dve.tensor_copy(flat(logits[:]), r_bank[:, 0:TC * E]))
                apart(dve)
                step(*(dve.max(top[:, c], logits[:, c]) for c in range(TC)))
                dve.tensor_tensor(gap[:], top[:, :, 1], top[:, :, 0], ALU.subtract).then_inc(gap_done, 1)
                step(*(dve.max_index(top_i[:, c], top[:, c], logits[:, c]) for c in range(TC)))
                step(dve.tensor_copy(choice[:].rearrange("p (c k) -> p c k", k=TOP_K), top_i[:, :, 0:TOP_K]))
                dve.wait_ge(counts_step, n * TC + 1)
                dve.tensor_tensor(onehot[:], iota_e[:].unsqueeze(1).broadcast_to((P, TC * TOP_K, E)),
                                  choice[:].unsqueeze(2).broadcast_to((P, TC * TOP_K, E)), ALU.is_equal
                                  ).then_inc(onehot_done, 1)
                assert done[0] == ROUTE

            PLACE = 9

            def place(n, p):
                done = [0]

                def step(*several):
                    for ins in several:
                        ins.then_inc(place_step, 1)
                        done[0] += 1
                    dve.wait_ge(place_step, n * PLACE + done[0])

                dve.wait_ge(ratio_done, n + 1)
                dve.wait_ge(pos_done, n + 1)
                step(dve.tensor_tensor(placed[:], r_bank[:, 64:64 + TC * TOP_K * E].rearrange(
                         "p (c e) -> p c e", e=E), onehot[:], ALU.mult),
                     dve.tensor_scalar(ratio1[:], ratio[:], 1.0, None, ALU.add),
                     dve.scalar_tensor_tensor(base[:], choice[:], float(ROWS), k_offset[:], ALU.mult, ALU.add))
                step(dve.tensor_reduce(pos[:], placed[:], AX_X, ALU.add),
                     dve.reciprocal(wts[:, :, 0], ratio1[:]))
                step(dve.tensor_tensor(base_k[:], base[:], pos[:], ALU.add),
                     dve.tensor_scalar(valid[:], pos[:], float(CAP), None, ALU.is_lt),
                     dve.tensor_tensor(wts[:, :, 1], ratio[:], wts[:, :, 0], ALU.mult))
                step(dve.scalar_tensor_tensor(moved[:], base_k[:], float(-SLOTS), valid[:], ALU.add, ALU.mult))
                dve.tensor_scalar(slot[:, p], moved[:], float(SLOTS), None, ALU.add).then_inc(slot_done, 1)
                dve.wait_ge(wts_kept, n + 1)
                dve.tensor_scalar(wts_g[:], wts[:], tanhs[:, 1:2], None, ALU.mult).then_inc(wts_done, 1)
                assert done[0] == PLACE

            dve.wait_ge(tanh_done, 1)
            dve.wait_ge(consts, 1)
            half = [None]

            def group(g, p, y, tail, ln, more):
                start = isinstance(g, int) and g == 0
                gh = g // 2 if isinstance(g, int) else half[0]
                for i in range(HALVES):
                    u = g * HALVES + i
                    row_recip(u, i)
                    if ln and i == 7:
                        xt_rest(g + 2, p, r_bank)
                    if more:
                        q_rest(g + 1, 1 - p, i)
                    if not (start and i < 2):
                        px_rest(u - 2, p if i >= 2 else 1 - p, (i - 2) % HALVES)
                    if not (not more and i == 7):
                        row_max(u + 1, i + 1, start and i < 1)
                    if not (start and i < 1):
                        probs_rest(u - 1, i - 1)
                    if tail and i == 0:
                        residual(g - 2, p, gh - 1)
                    if tail and i == 1:
                        token_norm(g - 2, p)
                    if ln and i == 1:
                        ln_stats(g + 2, p, gh + 2)
                    if more and i == 3:
                        group_mask(g + 1, 1 - p)
                    if tail and i == 3:
                        route(g - 2)
                    if ln and i == 2:
                        ln_normalise(g + 2, p)
                    if tail and i == 5:
                        place(g - 2, p)

            row_max(0, 0, True)

            group(0, 0, False, False, True, True)
            group(1, 1, True, False, True, True)
            with dve.Fori(1, NG // 2 - 1) as it:
                half[0] = it
                group(it * 2, 0, True, True, True, True)
                group(it * 2 + 1, 1, True, True, True, True)
            group(NG - 2, 0, True, True, False, True)
            group(NG - 1, 1, True, True, False, False)
            residual(NG - 2, 0, NG // 2 - 1)
            px_rest(LAST - 2, 1, HALVES - 2)
            probs_rest(LAST - 1, 1)
            token_norm(NG - 2, 0)
            px_rest(LAST - 1, 1, HALVES - 1)
            route(NG - 2)
            place(NG - 2, 0)

            def turn_rest(e, p, j):
                dst, hi = turned_into(1, p, j), turned_into(0, p, j)
                rest(dst, turn_bank(e, j)[:, 0:dst.shape[1]], hi, turned_hi, e * TURNS + j + 1, turned_lo)

            turn_rest(0, 0, 0)
            residual(NG - 1, 1, NG // 2 - 1)
            turn_rest(0, 0, 1)
            token_norm(NG - 1, 1)
            turn_rest(0, 0, 2)
            route(NG - 1)
            place(NG - 1, 1)
            turn_rest(0, 0, 3)
            turn_rest(0, 0, 4)

            def hidden_rest(e, f):
                rest(hid[:, 1, 1, f], hid_full[:, f], hid[:, 1, 0, f], hid_hi, e * UNITS + FC + f + 1, hid_lo[1])

            def copy_rows(e, p, piece):
                dve.wait_ge(ye_done, e * 2 + piece + 1)
                dst = flat(ye[:, p, 4 * piece:min(SC, 4 * piece + 4)])
                dve.tensor_copy(dst, BACK_BANK[piece][:, 0:dst.shape[1]]).then_inc(ye_copied, 1)

            def expert(e, p, number):
                first = isinstance(e, int) and e == 0
                for u in range(UNITS):
                    dve.wait_ge(silu_done, e * UNITS + u + 1)
                    if u >= FC:
                        dve.wait_ge(hid_lo[0], e * FC + u - FC + 1)
                    dve.tensor_tensor(hid_full[:, u % 4], silu[:, u % 2], q_bank[u % 2][:, 0:CAP], ALU.mult
                                      ).then_inc(hid_done, 1)
                    if u == 0 and not first:
                        hidden_rest(e - 1, FC - 1)
                    if u > FC:
                        hidden_rest(e, u - FC - 1)
                    if u == 3 and not first and not (isinstance(e, int) and e == 1):
                        dve.wait_ge(ye_free, e - 1)
                    if u in (3, 4) and not first:
                        copy_rows(e - 1, 1 - p, u - 3)
                    if number is not None and u in TURN_AFTER:
                        turn_rest(e + 1, 1 - p, TURN_AFTER[u])
                if not first:
                    dve.wait_ge(ye_free, e)
                dve.tensor_tensor(row_i[:, p], xe[:, p, :, D], row_offset[:], ALU.add).then_inc(rows_done, 1)

            experts(dve, expert)
            hidden_rest(E - 1, FC - 1)
            dve.wait_ge(ye_free, E - 1)
            copy_rows(E - 1, 1, 0)
            copy_rows(E - 1, 1, 1)

            dve.wait_ge(in_x1, 16)
            dve.wait_ge(wts_kept, NG + 1)
            for r in range(4):
                dve.wait_ge(picked[r], 16 * TOP_K)
                for c in range(4 * r, 4 * r + 4):
                    dve.scalar_tensor_tensor(part[:, c], y_pick[:, 0, c], wts_all[:, c, 0:1], x1_all[:, c],
                                             ALU.mult, ALU.add).then_inc(part_done, 1)
                dve.wait_ge(part_done, 4 * r + 4)
                for c in range(4 * r, 4 * r + 4):
                    dve.scalar_tensor_tensor(final[:, c], y_pick[:, 1, c], wts_all[:, c, 1:2], part[:, c],
                                             ALU.mult, ALU.add).then_inc(final_done, 1)


_INS = ['x', 'ctx_1024', 'mask_BxS2_bk0', 'g_xattn', 'g_ffn', 'L0_xattn_g1', 'L0_xattn_b1', 'L0_xattn_g2',
        'L0_xattn_b2', 'L0_xattn_Wq', 'L0_xattn_Wkv', 'L0_xattn_Wout', 'L0_ffn_gate_w', 'L0_ffn_wi_gate',
        'L0_ffn_wi_up', 'L0_ffn_wo']
_OUT = ((32, 64, 128), 'float32')


def kernel(**inputs):
    import numpy as _np
    import concourse.bacc as _bacc
    from concourse import mybir as _mybir
    from concourse.bass_utils import run_bass_kernel_spmd as _run

    nc = _bacc.Bacc("TRN2", target_bir_lowering=False, num_devices=1)
    arrays, args = {}, []
    for name in _INS:
        a = _np.ascontiguousarray(inputs[name])
        arrays[f"in_{name}_dram"] = a
        args.append(nc.dram_tensor(f"in_{name}_dram", a.shape, _mybir.dt.from_np(a.dtype), kind="ExternalInput").ap())
    out = nc.dram_tensor("out_0_dram", _OUT[0], _mybir.dt.from_np(_np.dtype(_OUT[1])), kind="ExternalOutput").ap()
    flamingo_block(nc, *args, out)
    r = _run(nc, [arrays], core_ids=[0])
    return r.results[0]["out_0_dram"]
```

```python
from contextlib import ExitStack

import numpy as np

import concourse.bass as bass
from concourse import mybir

F32 = mybir.dt.float32
F32R = mybir.dt.float32r
BF16 = mybir.dt.bfloat16
U32 = mybir.dt.uint32
I32 = mybir.dt.int32
U8 = mybir.dt.uint8
ALU = mybir.AluOpType
ACT = mybir.ActivationFunctionType
AX_X = mybir.AxisListType.X

P = 128
B, S, D = 32, 64, 128
HEADS, DH = 16, 64
EPS = 1e-5
E, F = 8, 512
TOP_K = 2
N = B * S
CAP = max(int(N / E * 1.25), 1)
ROWS = TOP_K * CAP
SLOTS = E * ROWS
SCALE = 1.0 / float(DH) ** 0.5
MASKED = 1e30

GB = 4
NG = B // GB
HALVES = 2 * GB
PAIRS = 4
GT = GB * S
TC = GT // P
ROW = D + 1
EMPTY = float(1 << 22)
FC = F // P
SC = ROWS // P
NT = N // P
HEADS_OF_SLOT = {1: (0, 2), 2: (2, 4), 3: (4, 6), 4: (6, 8), 5: (8, 11), 6: (11, 14), 7: (14, 16)}
HEADS_OF_SLOT_LAST = {1: (0, 4), 2: (4, 8), 3: (8, 11), 4: (11, 14), 5: (14, 16)}
assert ROWS % P == 0 and CAP <= 512 and NG % 2 == 0


def flamingo_block(nc, x, ctx_in, mask, g_xattn, g_ffn, g1, b1, g2, b2, Wq, Wkv, Wout,
                   gate_w, wi_gate, wi_up, wo, out):
    with ExitStack() as ctx:
        def sb(name, shape, dt=F32, scope=ctx):
            return scope.enter_context(nc.sbuf_tensor(name, shape, dt))

        def bytes_of(buffers):
            return sum(4 * int(np.prod(b.shape[1:])) for b in buffers)

        def bank(name):
            return ctx.enter_context(nc.psum_tensor(name, [P, 512], F32))

        def sem(name):
            return ctx.enter_context(nc.semaphore(name))

        x_flat = x.rearrange("b s d -> (b s) d")
        out_flat = out.rearrange("b s d -> (b s) d")
        x_slots = nc.dram_tensor("x_slots", (SLOTS, ROW), F32).ap()
        y_tokens = nc.dram_tensor("y_tokens", (TOP_K * N, D), F32).ap()
        x1_tokens = nc.dram_tensor("x1_tokens", (N, D), F32).ap()

        ident = sb("ident", [P, P])
        before = sb("before", [P, P], BF16)
        ones = sb("ones", [P, P], BF16)
        iota_i = sb("iota_i", [P, E], I32)
        iota_e = sb("iota_e", [P, E])
        token_i = sb("token_i", [P, NT], I32)
        token_f = sb("token_f", [P, NT])
        k_offset = sb("k_offset", [P, TC * TOP_K])
        row_offset = sb("row_offset", [P, SC])
        minus_half = sb("minus_half", [P, GB])
        var_scale = sb("var_scale", [P, 1])
        var_eps = sb("var_eps", [P, 1])
        empty = sb("empty", [P, ROW])
        gate_t = sb("gate_t", [P, E])
        affine = sb("affine", [P, 2, D])
        gains = sb("gains", [P, 2])
        tanhs = sb("tanhs", [P, 2])
        A = sb("A", [P, 2, HEADS, D], F32R)
        Bw = sb("Bw", [P, 2, HEADS, D], F32R)
        tok = sb("tok", [P, 2, GB, D])
        X = sb("X", [P, 2, 2, GB, D], F32R)
        XT = sb("XT", [P, 2, 2, GB, P], F32R)
        stats = sb("stats", [P, GB, 6])
        moments = sb("moments", [P, GB, 2])
        var_adj = sb("var_adj", [P, GB])
        rstd = sb("rstd", [P, GB])
        mask_u8 = sb("mask_u8", [1, 2, GT], U8)
        mask_g = sb("mask_g", [1, 2, GB, S], BF16)
        neg_max = sb("neg_max", [P, 2, PAIRS])
        sums = sb("sums", [P, 2, PAIRS])
        rsums = sb("rsums", [P, 2, PAIRS])
        probs = sb("probs", [P, 2, PAIRS, P])
        probs_t = sb("probs_t", [P, 2, 2, 512], F32R)
        yt = sb("yt", [P, TC, P])
        x1 = sb("x1", [P, 2, TC, D])
        t_stats = sb("t_stats", [P, TC, 6])
        t_moments = sb("t_moments", [P, TC, 2])
        t_var = sb("t_var", [P, TC])
        t_rstd = sb("t_rstd", [P, TC])
        xn = sb("xn", [P, 2, TC, ROW])
        xn_t = sb("xn_t", [P, TC, P])
        logits = sb("logits", [P, TC, E])
        top = sb("top", [P, TC, 8])
        top_i = sb("top_i", [P, TC, 8], U32)
        choice = sb("choice", [P, TC * TOP_K])
        onehot = sb("onehot", [P, TC * TOP_K, E], BF16)
        counts = sb("counts", [P, TOP_K * E], BF16)
        placed = sb("placed", [P, TC * TOP_K, E])
        pos = sb("pos", [P, TC * TOP_K])
        base = sb("base", [P, TC * TOP_K])
        base_k = sb("base_k", [P, TC * TOP_K])
        valid = sb("valid", [P, TC * TOP_K])
        moved = sb("moved", [P, TC * TOP_K])
        slot = sb("slot", [P, 2, TC * TOP_K], U32)
        gap = sb("gap", [P, TC])
        ratio = sb("ratio", [P, TC])
        ratio1 = sb("ratio1", [P, TC])
        wts = sb("wts", [P, TC, TOP_K])
        wts_g = sb("wts_g", [P, TC, TOP_K])
        wts_all = sb("wts_all", [P, NT, TOP_K])
        row_i = sb("row_i", [P, 2, SC], U32)

        with ExitStack() as first:
            sb("px_of_parity_0", [P, 2, GB, HEADS, S], F32R, first)
            wq_sb = sb("wq_sb", [P, HEADS * DH], F32, first)
            wkv_sb = sb("wkv_sb", [P, 2 * HEADS * DH], F32, first)
            wout_sb = sb("wout_sb", [P, HEADS // 2, D], F32, first)
            gate_sb = sb("gate_sb", [E, D], F32, first)
            w_t = sb("w_t", [P, 3 * HEADS // 2, P], F32, first)
        with ExitStack() as second:
            px = sb("px", [P, 2, 2, GB, HEADS, S], F32R, second)
            q = sb("q", [P, 2, 2, GB, HEADS, S], F32R, second)
        with ExitStack() as third:
            hid = sb("hid", [P, TOP_K, 2, FC, CAP], F32R, third)
            hid_full = sb("hid_full", [P, 4, CAP], F32, third)
            yet = sb("yet", [P, ROWS], F32, third)
            ye = sb("ye", [P, 2, SC, D], F32, third)
            silu = sb("silu", [P, 2, CAP], F32, third)
            xe_t = sb("xe_t", [P, 2, 2, SC * P], F32R, third)
            xe = sb("xe", [P, 2, SC, ROW], F32, third)
            px_bytes = 2 * 2 * GB * HEADS * S * 4
            used = (hid, hid_full, yet, ye, silu, xe_t, xe)
            sb("rest_of_px", [P, px_bytes - bytes_of(used)], U8, third)
            ewt = sb("ewt", [P, 2, 3, 2, FC, P], F32R, third)
            ew = sb("ew", [P, 2, 3, FC, P], F32, third)
            x1_all = sb("x1_all", [P, NT, D], F32, third)
        with ExitStack() as fourth:
            y_pick = sb("y_pick", [P, TOP_K, NT, D], F32, fourth)
            part = sb("part", [P, NT, D], F32, fourth)
            scaled = sb("scaled", [P, NT, D], F32, fourth)
            final = sb("final", [P, NT, D], F32, fourth)

        sc_bank = [bank("sc0"), bank("sc1")]
        tr_bank = bank("tr")
        px_bank = bank("pxb")
        q_bank = [bank("q0"), bank("q1")]
        y_bank = bank("yb")
        r_bank = bank("rb")

        in_q, in_k, in_v, in_wout = sem("in_q"), sem("in_k"), sem("in_v"), sem("in_wout")
        in_affine, in_small = sem("in_affine"), sem("in_small")
        in_tok = [sem("in_tok0"), sem("in_tok1")]
        in_resid = [sem("in_resid0"), sem("in_resid1")]
        empty_ready, slots_empty = sem("empty_ready"), sem("slots_empty")
        const_step, consts = sem("const_step"), sem("consts")
        gate_copied, tanh_done = sem("gate_copied"), sem("tanh_done")
        wt_done, wt_copied = sem("wt_done"), sem("wt_copied")
        ab_done, ab_hi, ab_lo = sem("ab_done"), sem("ab_hi"), sem("ab_lo")
        gate_done = sem("gate_done")
        stats_step, rstd_step = sem("stats_step"), sem("rstd_step")
        normed_done, scaled_done, tok_done = sem("normed_done"), sem("scaled_done"), sem("tok_done")
        X_hi, X_lo = sem("X_hi"), sem("X_lo")
        xt_done, xt_hi, xt_lo = sem("xt_done"), sem("xt_hi"), sem("xt_lo")
        q_done, q_hi, q_lo = sem("q_done"), sem("q_hi"), sem("q_lo")
        mask_ready = sem("mask_ready")
        s_done, max_done, exp_done = sem("s_done"), sem("max_done"), sem("exp_done")
        recip_done, norm_done = sem("recip_done"), sem("norm_done")
        tr_done, tr_hi, tr_lo = sem("tr_done"), sem("tr_hi"), sem("tr_lo")
        px_done, px_hi, px_lo = sem("px_done"), sem("px_hi"), sem("px_lo")
        y_done, y_copied, yt_done = sem("y_done"), sem("y_copied"), sem("yt_done")
        x1_done, t_stats_step, t_rstd_step = sem("x1_done"), sem("t_stats_step"), sem("t_rstd_step")
        xn_done, xnt_done, xnt_copied = sem("xn_done"), sem("xnt_done"), sem("xnt_copied")
        logits_done, route_step, place_step = sem("logits_done"), sem("route_step"), sem("place_step")
        gap_done, ratio_done, wts_done = sem("gap_done"), sem("ratio_done"), sem("wts_done")
        onehot_done, pos_done, counts_step = sem("onehot_done"), sem("pos_done"), sem("counts_step")
        slot_done = sem("slot_done")
        x1_stored, in_x1, wts_kept = [sem("x1_stored0"), sem("x1_stored1")], sem("in_x1"), sem("wts_kept")
        scattered, xn_free = [sem("scattered0"), sem("scattered1")], sem("xn_free")
        in_ew = [sem("in_ew0"), sem("in_ew1")]
        in_xe = [sem("in_xe0"), sem("in_xe1")]
        turned, turned_hi, turned_lo, rows_done = sem("turned"), sem("turned_hi"), sem("turned_lo"), sem("rows_done")
        gu_done, silu_done, hid_done = sem("gu_done"), sem("silu_done"), sem("hid_done")
        hid_hi, hid_lo = sem("hid_hi"), [sem("hid_lo_first"), sem("hid_lo_second")]
        yet_done, yet_copied, ye_done = sem("yet_done"), sem("yet_copied"), sem("ye_done")
        ye_copied, ye_free, y_sent = sem("ye_copied"), sem("ye_free"), sem("y_sent")
        waits_met = sem("waits_met")
        picked = [sem(f"picked{r}") for r in range(4)]
        first_part_done, second_part_done = sem("first_part_done"), sem("second_part_done")
        final_done, last_quarter_done, stored = sem("final_done"), sem("last_quarter_done"), sem("stored")

        def apart(eng):
            eng.sem_inc(waits_met, 1)

        def schedule(eng, body):
            body(0, 0, 0, False, False, True, True)
            body(1, 0, 1, True, False, True, True)
            with eng.Fori(1, NG // 2 - 1) as it:
                body(it * 2, it, 0, True, True, True, True)
                body(it * 2 + 1, it, 1, True, True, True, True)
            body(NG - 2, NG // 2 - 1, 0, True, True, False, True)
            body(NG - 1, NG // 2 - 1, 1, True, True, False, False)

        def experts(eng, body):
            body(0, 0, 1)
            body(1, 1, 2)
            with eng.Fori(1, E // 2 - 1) as it:
                body(it * 2, 0, it + 1)
                body(it * 2 + 1, 1, it + 2)
            body(E - 2, 0, E // 2)
            body(E - 1, 1, None)

        TURNS = 5
        TURN_AFTER = {0: 0, 2: 1, 3: 2, 5: 3, 6: 4}
        TURN_BANK = (tr_bank, r_bank, tr_bank, tr_bank, r_bank)
        DOWN_BEHIND = 3
        BACK = ((0, 2), (2, SC))
        Y_BANK = (px_bank, y_bank)
        UNITS = TOP_K * FC

        def query_bank(n, k):
            if isinstance(n, int) and n == 0:
                return (q_bank[0], q_bank[1], tr_bank, px_bank)[k % 4]
            return q_bank[k % 2]

        def setup_bank(k):
            return (sc_bank[0], sc_bank[1], tr_bank, px_bank)[k] if k < 4 else (y_bank, r_bank)[k % 2]

        def flat(ap):
            names = "abcdef"[:ap.ndim - 1]
            return ap.rearrange(f"p {' '.join(names)} -> p ({' '.join(names)})")

        def turned_into(part, p, j):
            if j < 3:
                return flat(ewt[:, p, j, part])
            return xe_t[:, p, part, 0:512] if j == 3 else xe_t[:, p, part, 512:ROWS]

        def turn_bank(e, j):
            if isinstance(e, int) and e == 0:
                return (sc_bank[0], sc_bank[1], q_bank[0], r_bank, tr_bank)[j]
            return TURN_BANK[j]

        LAST = NG * HALVES

        block = ctx.enter_context(nc.Block())

        @block.sync
        def _(sp):
            def load_tok(n, p):
                sp.dma_start(tok[0:S, p], ctx_in[n * GB:(n + 1) * GB].rearrange("b s d -> s b d")
                             ).then_inc(in_tok[p], 16)
                sp.dma_start(tok[S:P, p], x[n * GB:(n + 1) * GB].rearrange("b s d -> s b d")
                             ).then_inc(in_tok[p], 16)
                sp.dma_start(mask_u8[:, p], mask[n * GB:(n + 1) * GB].rearrange("b s -> (b s)").unsqueeze(0)
                             ).then_inc(in_tok[p], 16)

            def load_resid(n, p):
                sp.dma_start(x1[:, p], x_flat[n * GT:(n + 1) * GT, :].rearrange("(c p) d -> p c d", p=P)
                             ).then_inc(in_resid[p], 16)

            sp.dma_start(wq_sb[:], Wq).then_inc(in_q, 16)
            load_tok(0, 0)
            sp.dma_start(wkv_sb[:, 0:HEADS * DH], Wkv[:, 0:HEADS * DH]).then_inc(in_k, 16)
            for j, g in enumerate((g1, b1)):
                sp.dma_start(affine[0:S, j], g.partition_broadcast(S)).then_inc(in_affine, 16)
            for j, g in enumerate((g2, b2)):
                sp.dma_start(affine[S:P, j], g.partition_broadcast(S)).then_inc(in_affine, 16)
            load_tok(1, 1)
            sp.dma_start(wkv_sb[:, HEADS * DH:], Wkv[:, HEADS * DH:]).then_inc(in_v, 16)
            sp.dma_start(wout_sb[:], Wout.rearrange("(c p) e -> p c e", p=P)).then_inc(in_wout, 16)
            load_resid(0, 0)
            load_resid(1, 1)
            sp.wait_ge(empty_ready, 2)
            sp.dma_start(x_slots.rearrange("(c p) d -> p c d", p=P),
                         empty[:].unsqueeze(1).broadcast_to((P, SLOTS // P, ROW))).then_inc(slots_empty, 16)
            sp.dma_start(y_tokens.rearrange("(c p) d -> p c d", p=P),
                         empty[:, 0:D].unsqueeze(1).broadcast_to((P, TOP_K * NT, D))).then_inc(slots_empty, 16)

            for n in range(2, 5):
                sp.wait_ge(xt_done, n - 1)
                sp.wait_ge(X_lo, n - 1)
                sp.wait_ge(mask_ready, n - 1)
                load_tok(n, n % 2)

            def store_x1(n, p):
                sp.wait_ge(x1_done, n + 1)
                sp.dma_start(x1_tokens[n * GT:(n + 1) * GT, :].rearrange("(c p) d -> p c d", p=P), x1[:, p]
                             ).then_inc(x1_stored[p], 16)

            for n in range(2, NG):
                p = n % 2
                store_x1(n - 2, p)
                if n + 3 < NG:
                    sp.wait_ge(xt_done, n + 2)
                    sp.wait_ge(X_lo, n + 2)
                    sp.wait_ge(mask_ready, n + 2)
                    load_tok(n + 3, 1 - p)
                sp.wait_ge(x1_stored[p], n // 2 * 16)
                sp.wait_ge(xn_done, (n - 1) * (TC + 1))
                load_resid(n, p)
                sp.wait_ge(scattered[p], n // 2 * 16 * TC * TOP_K)
                sp.sem_inc(xn_free, 1)

            def load_expert(e, p):
                for j, w in enumerate((wi_gate, wi_up)):
                    sp.dma_start(ew[:, p, j], w[bass.ds(e, 1)].rearrange("o (c p) d -> p (o c) d", p=P)
                                 ).then_inc(in_ew[p], 16)
                sp.dma_start(ew[:, p, 2], wo[bass.ds(e, 1)].rearrange("o d (c f) -> d (o c) f", c=FC)
                             ).then_inc(in_ew[p], 16)

            def load_inputs(e, p):
                sp.dma_start(xe[:, p], x_slots[bass.ds(e * ROWS, ROWS), :].rearrange("(c p) d -> p c d", p=P)
                             ).then_inc(in_xe[p], 16)

            sp.wait_ge(s_done, LAST)
            load_expert(0, 0)
            load_expert(1, 1)
            store_x1(NG - 2, 0)
            store_x1(NG - 1, 1)
            for p in range(2):
                sp.wait_ge(scattered[p], 16 * TOP_K * NT // 2)
            load_inputs(0, 0)
            load_inputs(1, 1)
            for p in range(2):
                sp.wait_ge(x1_stored[p], NG // 2 * 16)
            sp.dma_start(x1_all[:], x1_tokens.rearrange("(c p) d -> p c d", p=P)).then_inc(in_x1, 16)

            def next_expert(e, p):
                sp.wait_ge(turned, e * TURNS + TURNS)
                load_expert(e + 2, p)
                sp.wait_ge(rows_done, e + 1)
                load_inputs(e + 2, p)

            with sp.Fori(0, E // 2 - 1) as it:
                next_expert(it * 2, 0)
                next_expert(it * 2 + 1, 1)

            sp.wait_ge(y_sent, 16 * SC * E)
            for r in range(4):
                for k in range(TOP_K):
                    row = k * N + r * 512
                    sp.dma_start(y_pick[:, k, 4 * r:4 * r + 4], y_tokens[row:row + 512, :].rearrange(
                        "(c p) d -> p c d", p=P)).then_inc(picked[r], 16)
            for r in range(4):
                if r < 3:
                    sp.wait_ge(final_done, r + 1)
                else:
                    sp.wait_ge(last_quarter_done, 1)
                sp.dma_start(out_flat[r * 512:(r + 1) * 512, :].rearrange("(c p) d -> p c d", p=P),
                             final[:, 4 * r:4 * r + 4]).then_inc(stored, 16)
            sp.wait_ge(stored, 64)

        @block.gpsimd
        def _(pool):
            count = [0]

            def const(ins):
                ins.then_inc(const_step, 1)
                count[0] += 1

            for s in (wts_kept, counts_step, y_copied):
                pool.sem_inc(s, 1)
            pool.sem_inc(xn_free, 2)
            const(pool.memset(ident[:], 0.0))
            const(pool.memset(before[:], 0.0))
            pool.wait_ge(const_step, 2)
            const(pool.affine_select(out=ident[:], in_=ident[:], compare_op=ALU.not_equal, fill=1.0, base=0,
                                     pattern=[[-1, P]], channel_multiplier=1))
            const(pool.affine_select(out=before[:], in_=before[:], compare_op=ALU.is_ge, fill=1.0, base=0,
                                     pattern=[[-1, P]], channel_multiplier=1))
            const(pool.memset(var_scale[:], 1.0))
            const(pool.memset(var_eps[:], EPS))
            pool.wait_ge(const_step, count[0])
            const(pool.memset(var_scale[S:P], 1.0 + EPS))
            const(pool.memset(var_eps[S:P], EPS * EPS))
            pool.wait_ge(const_step, count[0])
            const(pool.memset(ones[:], 1.0))
            pool.memset(empty[:, 0:D], 0.0).then_inc(empty_ready, 1)
            pool.memset(empty[:, D:ROW], EMPTY).then_inc(empty_ready, 1)
            const(pool.memset(counts[:], 0.0))
            const(pool.memset(minus_half[:], -0.5))
            const(pool.iota(iota_i[:], [[1, E]], base=0, channel_multiplier=0))
            const(pool.iota(token_i[:], [[P, NT]], base=0, channel_multiplier=1))
            for k in range(TC * TOP_K):
                const(pool.memset(k_offset[:, k:k + 1], float(k % TOP_K * CAP)))
            const(pool.memset(row_offset[:], 0.0))
            pool.wait_ge(const_step, count[0])
            const(pool.affine_select(out=row_offset[:], in_=row_offset[:], compare_op=ALU.is_gt, fill=float(N),
                                     base=CAP, pattern=[[-P, SC]], channel_multiplier=-1))
            pool.wait_ge(const_step, count[0])
            const(pool.tensor_copy(token_f[:], token_i[:]))
            const(pool.tensor_copy(iota_e[:], iota_i[:]))
            pool.wait_ge(const_step, count[0])
            pool.sem_inc(consts, 1)

            def ln_rstd(n):
                pool.wait_ge(stats_step, n * 2 * GB + 2 * GB)
                apart(pool)
                pool.tensor_scalar(var_adj[:], moments[:, :, 1], var_scale[:, 0:1], var_eps[:, 0:1],
                                   ALU.mult, ALU.add).then_inc(rstd_step, 1)
                pool.wait_ge(rstd_step, n * 2 + 1)
                pool.tensor_tensor(rstd[:], var_adj[:], minus_half[:], ALU.pow).then_inc(rstd_step, 1)

            def ln_gain(n, p):
                pool.wait_ge(normed_done, n + 1)
                pool.tensor_tensor(tok[:, p], tok[:, p], affine[:, 0:1, :].broadcast_to((P, GB, D)),
                                   ALU.mult).then_inc(scaled_done, 1)

            def ln_shift(n, p):
                pool.wait_ge(scaled_done, n + 1)
                pool.tensor_tensor(tok[:, p], tok[:, p], affine[:, 1:2, :].broadcast_to((P, GB, D)),
                                   ALU.add).then_inc(tok_done, 1)

            def split_tok(n, p):
                pool.wait_ge(X_hi, n + 1)
                pool.tensor_tensor(X[:, p, 1], tok[:, p], X[:, p, 0].bitcast(F32), ALU.subtract).then_inc(X_lo, 1)

            ln_rstd(0)
            pool.wait_ge(in_affine, 4 * 16)
            ln_gain(0, 0)
            ln_shift(0, 0)
            ln_rstd(1)
            ln_gain(1, 1)
            ln_shift(1, 1)
            split_tok(0, 0)

            def normalise(u, i):
                pool.wait_ge(recip_done, u + 1)
                pool.tensor_tensor(probs[:, i % 2], probs[:, i % 2],
                                   rsums[:, i % 2].unsqueeze(2).broadcast_to((P, PAIRS, P)), ALU.mult
                                   ).then_inc(norm_done, 1)

            def token_rstd(n):
                pool.wait_ge(t_stats_step, n * 2 * TC + 2 * TC)
                apart(pool)
                pool.tensor_scalar(t_var[:], t_moments[:, :, 1], EPS, None, ALU.add).then_inc(t_rstd_step, 1)
                pool.wait_ge(t_rstd_step, n * 2 + 1)
                pool.tensor_tensor(t_rstd[:], t_var[:], minus_half[:, 0:TC], ALU.pow).then_inc(t_rstd_step, 1)

            def number_tokens(n, p):
                pool.wait_ge(xn_free, n + 1)
                apart(pool)
                pool.tensor_copy(xn[:, p, :, D], token_f[:, bass.ds(n * TC, TC)]).then_inc(xn_done, 1)

            def count_tokens(n):
                pool.wait_ge(pos_done, n + 1)
                for c in range(TC):
                    pool.tensor_tensor(counts[:], counts[:], onehot[:, TOP_K * c:TOP_K * (c + 1), :].rearrange(
                        "p k e -> p (k e)"), ALU.add).then_inc(counts_step, 1)
                    pool.wait_ge(counts_step, n * TC + c + 2)
                pool.wait_ge(wts_done, n + 1)
                apart(pool)
                pool.tensor_copy(wts_all[:, bass.ds(n * TC, TC), :], wts_g[:]).then_inc(wts_kept, 1)

            def scatter(n, p, k):
                if k == 0:
                    pool.wait_ge(slot_done, n + 1)
                    apart(pool)
                for c in range(TC):
                    i = TOP_K * c + k
                    pool.indirect_dma_start(x_slots, bass.IndirectOffsetOnAxis(slot[:, p, i:i + 1], 0),
                                            xn[:, p, c], None, bounds_check=SLOTS - 1, oob_is_err=False
                                            ).then_inc(scattered[p], 16)

            def group(g, h, p, y, tail, ln, more):
                for i in range(HALVES):
                    normalise(g * HALVES + i, i)
                    if tail and i == 0:
                        token_rstd(g - 2)
                        number_tokens(g - 2, p)
                    if ln and i == 2:
                        ln_rstd(g + 2)
                    if more and i == 1:
                        split_tok(g + 1, 1 - p)
                    if ln and i == 4:
                        ln_gain(g + 2, p)
                    if ln and i == 5:
                        ln_shift(g + 2, p)
                    if tail and i == 5:
                        count_tokens(g - 2)
                    if tail and i == 6:
                        scatter(g - 2, p, 0)
                    if not more and i == 6:
                        token_rstd(g - 1)
                        number_tokens(g - 1, 1 - p)
                    if tail and i == 7:
                        scatter(g - 2, p, 1)
                if y and not tail:
                    pool.wait_ge(slots_empty, 32)

            schedule(pool, group)
            count_tokens(NG - 2)
            scatter(NG - 2, 0, 0)
            token_rstd(NG - 1)
            number_tokens(NG - 1, 1)
            scatter(NG - 2, 0, 1)
            scatter(NG - 1, 1, 0)
            scatter(NG - 1, 1, 1)
            count_tokens(NG - 1)

            def hidden_rest(e, f):
                pool.wait_ge(hid_hi, e * UNITS + f + 1)
                pool.tensor_tensor(hid[:, 0, 1, f], hid_full[:, f], hid[:, 0, 0, f].bitcast(F32),
                                   ALU.subtract).then_inc(hid_lo[0], 1)

            def send_rows(e, p, c):
                pool.indirect_dma_start(y_tokens, bass.IndirectOffsetOnAxis(row_i[:, p, c:c + 1], 0),
                                        ye[:, p, c], None, bounds_check=TOP_K * N - 1, oob_is_err=False
                                        ).then_inc(y_sent, 16)

            def send_piece(e, p, piece):
                pool.wait_ge(rows_done, e + 1)
                pool.wait_ge(ye_copied, e * 2 + piece + 1)
                apart(pool)
                for c in range(*BACK[piece]):
                    send_rows(e, p, c)

            def expert(e, p, number):
                first = isinstance(e, int) and e == 0
                if not first:
                    if not (isinstance(e, int) and e == 1):
                        pool.wait_ge(y_sent, (e - 1) * 16 * SC)
                    pool.sem_inc(ye_free, 1)
                for f in range(FC):
                    hidden_rest(e, f)
                    if f == 0 and not first:
                        send_piece(e - 1, 1 - p, 0)
                if not first:
                    send_piece(e - 1, 1 - p, 1)

            experts(pool, expert)
            pool.wait_ge(y_sent, (E - 1) * 16 * SC)
            send_piece(E - 1, 1, 0)
            send_piece(E - 1, 1, 1)
            for r in range(3):
                quarter = slice(4 * r, 4 * r + 4)
                pool.wait_ge(first_part_done, 4 * r + 4)
                pool.wait_ge(second_part_done, 4 * r + 4)
                pool.tensor_tensor(final[:, quarter], part[:, quarter], scaled[:, quarter], ALU.add
                                   ).then_inc(final_done, 1)

        @block.scalar
        def _(act):
            def copy_wt(k):
                act.wait_ge(wt_done, k + 1)
                act.copy(flat(w_t[:, 4 * k:4 * k + 4]), setup_bank(k)[:]).then_inc(wt_copied, 1)

            def xt_round(n, p, src):
                act.wait_ge(xt_done, n + 1)
                act.copy(flat(XT[:, p, 0]), src[:]).then_inc(xt_hi, 1)

            def X_round(n, p):
                if not (isinstance(n, int) and n < 2):
                    act.wait_ge(px_done, (n - 1) * HALVES)
                act.wait_ge(tok_done, n + 1)
                act.copy(X[:, p, 0], tok[:, p]).then_inc(X_hi, 1)

            def ab_round(k):
                act.wait_ge(ab_done, k + 1)
                h0 = 8 * (k % 4 // 2) + k % 2
                dst = (A if k < 4 else Bw)[:, 0, h0:h0 + 7:2]
                act.activation(dst, setup_bank(k)[:].rearrange("p (h d) -> p h d", h=4), ACT.Copy,
                               scale=SCALE if k < 4 else 1.0).then_inc(ab_hi, 1)

            def q_round(n, p, k):
                act.wait_ge(q_done, n * 8 + k + 1)
                act.copy(q[:, p, 0, :, 2 * k:2 * k + 2, :].rearrange("p b h s -> p h b s"),
                         query_bank(n, k)[:].rearrange("p (h b s) -> p h b s", h=2, b=GB)).then_inc(q_hi, 1)

            for k in range(4):
                copy_wt(k)
            act.dma_start(gate_sb[:], gate_w).then_inc(in_small, 16)
            act.dma_start(gains[:, 0:1], g_xattn.partition_broadcast(P)).then_inc(in_small, 16)
            act.dma_start(gains[:, 1:2], g_ffn.partition_broadcast(P)).then_inc(in_small, 16)
            for k in range(4):
                ab_round(k)
            xt_round(0, 0, r_bank)
            xt_round(1, 1, y_bank)
            for k in range(8):
                q_round(0, 0, k)
                if k == 3:
                    X_round(0, 0)
            copy_wt(4)
            copy_wt(5)
            act.wait_ge(in_small, 48)
            act.activation(tanhs[:], gains[:], ACT.Tanh).then_inc(tanh_done, 1)

            def softmax(u, i, early):
                r = i % 2
                act.wait_ge(max_done, u + 1)
                if not early:
                    act.wait_ge(tr_done, u - 1)
                for j in range(PAIRS):
                    act.activation(probs[:, r, j], sc_bank[r][:, j * P:(j + 1) * P], ACT.Exp,
                                   bias=neg_max[:, r, j:j + 1], accum_out=sums[:, r, j:j + 1]
                                   ).then_inc(exp_done, 1)

            def probs_round(v, i, early):
                act.wait_ge(tr_done, v + 1)
                if not early:
                    act.wait_ge(px_done, v - 1)
                act.copy(probs_t[:, i % 2, 0], tr_bank[:]).then_inc(tr_hi, 1)

            def px_round(v, p, i):
                b, hf = divmod(i, 2)
                act.wait_ge(px_done, v + 1)
                act.copy(flat(px[:, p, 0, b, 8 * hf:8 * hf + 8]), px_bank[:]).then_inc(px_hi, 1)

            def copy_y(n):
                act.wait_ge(y_done, n + 1)
                act.copy(flat(yt[:]), y_bank[:, 0:GT]).then_inc(y_copied, 1)

            def copy_xnt(n):
                act.wait_ge(xnt_done, n + 1)
                act.copy(flat(xn_t[:]), r_bank[:, 0:GT]).then_inc(xnt_copied, 1)

            def gate_ratio(n):
                act.wait_ge(gap_done, n + 1)
                act.activation(ratio[:], gap[:], ACT.Exp).then_inc(ratio_done, 1)

            def group(g, h, p, y, tail, ln, more):
                start = isinstance(g, int) and g == 0
                for i in range(HALVES):
                    u = g * HALVES + i
                    softmax(u, i, start and i < 2)
                    if ln and i == 7:
                        xt_round(g + 2, p, r_bank)
                    if not (start and i < 2):
                        px_round(u - 2, p if i >= 2 else 1 - p, (i - 2) % HALVES)
                    if not (start and i < 1):
                        probs_round(u - 1, (i - 1) % 2, start and i < 3)
                    if more:
                        q_round(g + 1, 1 - p, i)
                    if start and i < 4:
                        ab_round(4 + i)
                    if more and i == 1:
                        X_round(g + 1, 1 - p)
                    if tail and i == 2:
                        copy_xnt(g - 2)
                    if tail and i == 4:
                        gate_ratio(g - 2)
                    if y and i == (7 if more else 5):
                        copy_y(g - 1)

            schedule(act, group)

            def turn_round(e, p, j):
                act.wait_ge(turned, e * TURNS + j + 1)
                dst = turned_into(0, p, j)
                act.copy(dst, turn_bank(e, j)[:, 0:dst.shape[1]]).then_inc(turned_hi, 1)

            px_round(LAST - 2, 1, HALVES - 2)
            probs_round(LAST - 1, 1, False)
            copy_xnt(NG - 2)
            px_round(LAST - 1, 1, HALVES - 1)
            gate_ratio(NG - 2)
            copy_y(NG - 1)
            turn_round(0, 0, 0)
            turn_round(0, 0, 1)
            copy_xnt(NG - 1)
            turn_round(0, 0, 2)
            gate_ratio(NG - 1)
            turn_round(0, 0, 3)
            turn_round(0, 0, 4)

            def hid_round(e, u):
                k, f = divmod(u, FC)
                act.wait_ge(hid_done, e * UNITS + u + 1)
                act.copy(hid[:, k, 0, f], hid_full[:, u % 4]).then_inc(hid_hi, 1)

            def copy_yet(e, k):
                act.wait_ge(yet_done, e * TOP_K + k + 1)
                act.copy(yet[:, k * CAP:(k + 1) * CAP], Y_BANK[k][:, 0:CAP]).then_inc(yet_copied, 1)

            def expert(e, p, number):
                first = isinstance(e, int) and e == 0
                for u in range(UNITS):
                    act.wait_ge(gu_done, e * UNITS + u + 1)
                    act.activation(silu[:, u % 2], sc_bank[u % 2][:, 0:CAP], ACT.Silu).then_inc(silu_done, 1)
                    if not (first and u == 0):
                        if u == 0:
                            hid_round(e - 1, UNITS - 1)
                        else:
                            hid_round(e, u - 1)
                    if u == DOWN_BEHIND and not first:
                        copy_yet(e - 1, 1)
                    if u == DOWN_BEHIND + FC:
                        copy_yet(e, 0)
                    if number is not None and u in TURN_AFTER:
                        turn_round(e + 1, 1 - p, TURN_AFTER[u])

            experts(act, expert)
            hid_round(E - 1, UNITS - 1)
            copy_yet(E - 1, 1)
            act.wait_ge(wts_kept, NG + 1)
            for r in range(4):
                act.wait_ge(picked[r], 16 * TOP_K)
                for c in range(4 * r, 4 * r + 4):
                    act.activation(scaled[:, c], y_pick[:, 1, c], ACT.Copy, scale=wts_all[:, c, 1:2]
                                   ).then_inc(second_part_done, 1)

        @block.tensor
        def _(pe):
            def product(o, w, v, n, start=True, stop=True, **kw):
                for t, (a, b) in enumerate(((0, 0), (0, 1), (1, 0))):
                    mm = pe.matmul(o, w(a), v(b), start=start and t == 0, stop=stop and t == 2, **kw)
                return mm

            def transpose_w(k):
                for j in range(4):
                    c = 4 * k + j
                    src = wq_sb[:, c * P:(c + 1) * P] if c < 8 else wkv_sb[:, (c - 8) * P:(c - 7) * P]
                    mm = pe.transpose(setup_bank(k)[:, j * P:(j + 1) * P], src, ident[:])
                mm.then_inc(wt_done, 1)

            def transpose_tok(n, p, dst):
                pe.wait_ge(tok_done, n + 1)
                for b in range(GB):
                    mm = pe.transpose(dst[:, b * P:(b + 1) * P], tok[:, p, b], ident[:])
                mm.then_inc(xt_done, 1)

            def combine_weights(k):
                for j in range(4):
                    h = 8 * (k % 4 // 2) + 2 * j + k % 2
                    rows = slice(DH * (h % 2), DH * (h % 2) + DH)
                    if k < 4:
                        lhs, rhs = w_t[rows, h // 2], w_t[rows, 8 + h // 2]
                    else:
                        lhs, rhs = w_t[rows, 16 + h // 2], wout_sb[rows, h // 2]
                    mm = pe.matmul(setup_bank(k)[:, j * P:(j + 1) * P], lhs, rhs, start=True, stop=True)
                mm.then_inc(ab_done, 1)

            def project(n, p, k):
                if not (isinstance(n, int) and n == 0):
                    pe.wait_ge(q_lo, n * 8 + k - 1)
                elif k >= 4:
                    pe.wait_ge(q_lo, k - 3)
                for h in (2 * k, 2 * k + 1):
                    mm = product(query_bank(n, k)[:, (h % 2) * GT:(h % 2 + 1) * GT], lambda a: A[:, a, h],
                                 lambda b: XT[:, p, b, :, S:P], GT)
                mm.then_inc(q_done, 1)

            pe.wait_ge(const_step, 4)
            pe.wait_ge(in_q, 16)
            transpose_w(0)
            transpose_w(1)
            pe.wait_ge(in_k, 16)
            transpose_w(2)
            transpose_w(3)
            pe.wait_ge(wt_copied, 4)
            for k in range(4):
                combine_weights(k)
            pe.wait_ge(in_small, 48)
            pe.transpose(y_bank[:, 0:E], gate_sb[:], ident[0:E, 0:E]).then_inc(gate_done, 1)
            transpose_tok(0, 0, r_bank)
            pe.wait_ge(gate_copied, 1)
            transpose_tok(1, 1, y_bank)
            pe.wait_ge(ab_lo, 4)
            pe.wait_ge(xt_lo, 1)
            for k in range(8):
                project(0, 0, k)
                if k == 3:
                    pe.wait_ge(in_v, 16)
                    pe.wait_ge(xt_lo, 2)
                    transpose_w(4)
                    transpose_w(5)
            pe.wait_ge(consts, 1)
            pe.wait_ge(in_wout, 16)

            def scores(g, p, u, i, early):
                b, hf = divmod(i, 2)
                if i == 0:
                    pe.wait_ge(mask_ready, g + 1)
                if i < 2:
                    pe.wait_ge(q_lo, g * 8 + 4 * i + 4)
                if not early:
                    pe.wait_ge(exp_done, (u - 1) * PAIRS)
                s = sc_bank[i % 2][:].rearrange("p (j k) -> p j k", j=PAIRS)
                pe.matmul(s[:, :, 0:S], ones[0:1, :], mask_g[:, p, b:b + 1].broadcast_to((1, PAIRS, S)),
                          start=True, stop=False, skip_group_check=True)
                for j in range(PAIRS):
                    h = 2 * (PAIRS * hf + j)
                    mm = product(s[:, j], lambda a: flat(q[:, p, a, b, h:h + 2]), lambda c: XT[:, p, c, b], P,
                                 start=False, stop=j == PAIRS - 1, skip_group_check=True)
                mm.then_inc(s_done, 1)

            def transpose_probs(v, i, early):
                pe.wait_ge(norm_done, v + 1)
                if not early:
                    pe.wait_ge(tr_lo, v)
                for j in range(PAIRS):
                    mm = pe.transpose(tr_bank[:, j * P:(j + 1) * P], probs[:, i % 2, j], ident[:])
                mm.then_inc(tr_done, 1)

            def mix(v, g, p, i, early):
                pe.wait_ge(tr_lo, v + 1)
                if i == 0:
                    pe.wait_ge(X_lo, g + 1)
                if not early:
                    pe.wait_ge(px_lo, v)
                product(px_bank[:], lambda a: X[:, p, a, i // 2], lambda b: probs_t[:, i % 2, b], 512
                        ).then_inc(px_done, 1)

            def out_heads(n, p, h0, h1):
                if h0 == 0:
                    pe.wait_ge(px_lo, n * HALVES + HALVES - 1)
                if h0 <= HEADS // 2 < h1:
                    pe.wait_ge(px_lo, n * HALVES + HALVES)
                if h0 == 0:
                    pe.wait_ge(y_copied, n + 1)
                for h in range(h0, h1):
                    mm = product(y_bank[:, 0:GT], lambda a: Bw[:, a, h], lambda b: px[:, p, b, :, h], GT,
                                 start=h == 0, stop=h == HEADS - 1)
                if h1 == HEADS:
                    mm.then_inc(y_done, 1)

            def transpose_y(n):
                pe.wait_ge(y_copied, n + 2)
                for c in range(TC):
                    mm = pe.transpose(r_bank[:, c * P:(c + 1) * P], yt[:, c], ident[:])
                mm.then_inc(yt_done, 1)

            def transpose_xn(n, p):
                pe.wait_ge(xn_done, n * (TC + 1) + TC + 1)
                for c in range(TC):
                    mm = pe.transpose(r_bank[:, c * P:(c + 1) * P], xn[:, p, c, 0:D], ident[:])
                mm.then_inc(xnt_done, 1)

            def route_logits(n):
                pe.wait_ge(xnt_copied, n + 1)
                for c in range(TC):
                    mm = pe.matmul(r_bank[:, c * E:(c + 1) * E], xn_t[:, c], gate_t[:], start=True, stop=True)
                mm.then_inc(logits_done, 1)

            def positions(n):
                pe.wait_ge(onehot_done, n + 1)
                pe.wait_ge(counts_step, n * TC + 1)
                for c in range(TC):
                    o = r_bank[:, 64 + c * TOP_K * E:64 + (c + 1) * TOP_K * E]
                    hot = [flat(onehot[:, TOP_K * a:TOP_K * (a + 1)]) for a in range(c + 1)]
                    pe.matmul(o, before[:], hot[c], start=True, stop=False)
                    for a in range(c):
                        pe.matmul(o, ones[:], hot[a], start=False, stop=False)
                    mm = pe.matmul(o, ones[:], counts[:], start=False, stop=True)
                mm.then_inc(pos_done, 1)

            def group(g, h, p, y, tail, ln, more):
                start = isinstance(g, int) and g == 0
                for i in range(HALVES):
                    u = g * HALVES + i
                    scores(g, p, u, i, start and i < 2)
                    if start and i == 0:
                        pe.wait_ge(wt_copied, 6)
                    if ln and i == 7:
                        if tail:
                            pe.wait_ge(slot_done, g - 1)
                        transpose_tok(g + 2, p, r_bank)
                    if more:
                        if i == 0:
                            pe.wait_ge(xt_lo, g + 2)
                        project(g + 1, 1 - p, i)
                    if start and i < 4:
                        if i >= 2:
                            pe.wait_ge(ab_lo, 3 + i)
                        combine_weights(4 + i)
                    if tail and i == 3:
                        route_logits(g - 2)
                    if tail and i == 5:
                        positions(g - 2)
                    heads = HEADS_OF_SLOT if more else HEADS_OF_SLOT_LAST
                    if y and i in heads:
                        out_heads(g - 1, 1 - p, *heads[i])
                    if tail and i == 0:
                        transpose_y(g - 2)
                    if not (start and i < 2):
                        mix(u - 2, g, p if i >= 2 else 1 - p, (i - 2) % HALVES, start and i == 2)
                    if not (start and i < 1):
                        transpose_probs(u - 1, i - 1, start and i == 1)
                    if tail and i == 2:
                        transpose_xn(g - 2, p)
                    if not more and i == 6:
                        pe.wait_ge(slot_done, g - 1)
                        transpose_y(g - 1)

            schedule(pe, group)

            def turn(e, p, j, number):
                if not (isinstance(e, int) and e == 0):
                    if j in (1, 4) and not (isinstance(e, int) and e == 1):
                        pe.wait_ge(ye_copied, e * 2 - (3 if j == 1 else 2))
                    else:
                        pe.wait_ge(turned_lo, e * TURNS + (0, 0, 1, 3, 2)[j])
                if j == 0:
                    pe.wait_ge(in_ew[p], number * 48)
                if j == 3:
                    pe.wait_ge(in_xe[p], number * 16)
                chunks = (ew[:, p, j, c] for c in range(FC)) if j < 3 else (
                    xe[:, p, c, 0:D] for c in range((j - 3) * 4, min(SC, (j - 2) * 4)))
                for c, chunk in enumerate(chunks):
                    mm = pe.transpose(turn_bank(e, j)[:, c * P:(c + 1) * P], chunk, ident[:])
                mm.then_inc(turned, 1)

            mix(LAST - 2, NG - 1, 1, HALVES - 2, False)
            transpose_probs(LAST - 1, 1, False)
            transpose_xn(NG - 2, 0)
            out_heads(NG - 1, 1, 0, 4)
            mix(LAST - 1, NG - 1, 1, HALVES - 1, False)
            out_heads(NG - 1, 1, 4, HEADS // 2)
            route_logits(NG - 2)
            out_heads(NG - 1, 1, HEADS // 2, 3 * HEADS // 4)
            positions(NG - 2)
            out_heads(NG - 1, 1, 3 * HEADS // 4, HEADS)
            turn(0, 0, 0, 1)
            pe.wait_ge(slot_done, NG - 1)
            transpose_y(NG - 1)
            turn(0, 0, 1, 1)
            transpose_xn(NG - 1, 1)
            route_logits(NG - 1)
            turn(0, 0, 2, 1)
            positions(NG - 1)
            pe.wait_ge(slot_done, NG)
            turn(0, 0, 3, 1)
            turn(0, 0, 4, 1)

            def gate_up(e, p, u):
                k, f = divmod(u, FC)
                if not (isinstance(e, int) and e == 0 and u < 2):
                    pe.wait_ge(hid_done, e * UNITS + u - 1)
                for j, b in enumerate((sc_bank[u % 2], q_bank[u % 2])):
                    mm = product(b[:, 0:CAP], lambda a: ewt[:, p, j, a, f],
                                 lambda c: xe_t[:, p, c, k * CAP:(k + 1) * CAP], CAP)
                mm.then_inc(gu_done, 1)

            def down(e, p, k, f):
                pe.wait_ge(hid_lo[k], e * FC + f + 1)
                if f == 0 and not (isinstance(e, int) and e == 0):
                    pe.wait_ge(yet_copied, e * TOP_K + k - 1)
                mm = product(Y_BANK[k][:, 0:CAP], lambda a: ewt[:, p, 2, a, f], lambda b: hid[:, k, b, f], CAP,
                             start=f == 0, stop=f == FC - 1)
                if f == FC - 1:
                    mm.then_inc(yet_done, 1)

            def turn_back(e, piece, last=False):
                pe.wait_ge(yet_copied, e * TOP_K + piece + 1)
                if piece == 0 and not (isinstance(e, int) and e == E - 1):
                    pe.wait_ge(turned_lo, (e + 2) * TURNS)
                elif piece == 0:
                    pe.wait_ge(ye_copied, e * 2)
                elif last:
                    pe.wait_ge(ye_copied, e * 2 + 1)
                else:
                    pe.wait_ge(turned_lo, (e + 2) * TURNS + 2)
                for o, c in enumerate(range(*BACK[piece])):
                    mm = pe.transpose(r_bank[:, o * P:(o + 1) * P], yet[:, c * P:(c + 1) * P], ident[:])
                mm.then_inc(ye_done, 1)

            def expert(e, p, number):
                first = isinstance(e, int) and e == 0
                for u in range(UNITS):
                    if u in (0, FC):
                        pe.wait_ge(turned_lo, e * TURNS + TURNS - (u == 0))
                    gate_up(e, p, u)
                    if u >= DOWN_BEHIND:
                        down(e, p, *divmod(u - DOWN_BEHIND, FC))
                    elif not first:
                        down(e - 1, 1 - p, 1, FC - DOWN_BEHIND + u)
                    if number is not None and u in TURN_AFTER:
                        turn(e + 1, 1 - p, TURN_AFTER[u], number)
                    if u in (0, 4) and not first:
                        turn_back(e - 1, u // 4, last=number is None)

            experts(pe, expert)
            turn_back(E - 1, 0, last=True)
            for f in range(FC - DOWN_BEHIND, FC):
                down(E - 1, 1, 1, f)
            turn_back(E - 1, 1, last=True)

        @block.vector
        def _(dve):
            def ln_stats(n, p, loads):
                dve.wait_ge(in_tok[p], loads * 48)
                for b in range(GB):
                    dve.bn_stats(stats[:, b], tok[:, p, b]).then_inc(stats_step, 1)
                dve.wait_ge(stats_step, n * 2 * GB + GB)
                if not isinstance(n, int):
                    apart(dve)
                for b in range(GB):
                    dve.bn_aggr(moments[:, b], stats[:, b]).then_inc(stats_step, 1)

            def ln_normalise(n, p):
                dve.wait_ge(rstd_step, n * 2 + 2)
                for b in range(GB):
                    ins = dve.tensor_scalar(tok[:, p, b], tok[:, p, b], moments[:, b, 0:1], rstd[:, b:b + 1],
                                            ALU.subtract, ALU.mult)
                ins.then_inc(normed_done, 1)

            def rest(out_lo, full, hi, wait_for, value, done, scale=None):
                dve.wait_ge(wait_for, value)
                if scale is None:
                    dve.tensor_tensor(out_lo, full, hi.bitcast(F32), ALU.subtract).then_inc(done, 1)
                else:
                    dve.scalar_tensor_tensor(out_lo, full, scale, hi.bitcast(F32), ALU.mult, ALU.subtract
                                             ).then_inc(done, 1)

            def xt_rest(n, p, src):
                rest(flat(XT[:, p, 1]), src[:], flat(XT[:, p, 0]), xt_hi, n + 1, xt_lo)

            def group_mask(n, p):
                dve.tensor_scalar(mask_g[:, p].rearrange("a b s -> a (b s)"), mask_u8[:, p], MASKED, MASKED,
                                  ALU.mult, ALU.subtract).then_inc(mask_ready, 1)

            def q_rest(n, p, k):
                dve.wait_ge(q_hi, n * 8 + k + 1)
                for h in (2 * k, 2 * k + 1):
                    ins = dve.tensor_tensor(q[:, p, 1, :, h, :],
                                            query_bank(n, k)[:, (h % 2) * GT:(h % 2 + 1) * GT].rearrange(
                                                "p (b s) -> p b s", b=GB),
                                            q[:, p, 0, :, h, :].bitcast(F32), ALU.subtract)
                ins.then_inc(q_lo, 1)

            def ab_rest(k):
                dst = A if k < 4 else Bw
                h0 = 8 * (k % 4 // 2) + k % 2
                rest(dst[:, 1, h0:h0 + 7:2], setup_bank(k)[:].rearrange("p (h d) -> p h d", h=4),
                     dst[:, 0, h0:h0 + 7:2], ab_hi, k + 1, ab_lo, SCALE if k < 4 else None)

            ln_stats(0, 0, 1)
            group_mask(0, 0)
            ln_normalise(0, 0)
            for k in range(4):
                ab_rest(k)
                if k == 0:
                    ln_stats(1, 1, 1)
                if k == 1:
                    ln_normalise(1, 1)
            dve.wait_ge(gate_done, 1)
            dve.tensor_copy(gate_t[:], y_bank[:, 0:E]).then_inc(gate_copied, 1)
            xt_rest(0, 0, r_bank)
            xt_rest(1, 1, y_bank)
            for k in range(8):
                q_rest(0, 0, k)

            def row_max(u, i, early):
                dve.wait_ge(s_done, u + 1)
                if not early:
                    dve.wait_ge(norm_done, u - 1)
                dve.tensor_reduce(neg_max[:, i % 2], sc_bank[i % 2][:].rearrange("p (j k) -> p j k", j=PAIRS),
                                  AX_X, ALU.max, negate=True).then_inc(max_done, 1)

            def row_recip(u, i):
                dve.wait_ge(exp_done, (u + 1) * PAIRS)
                dve.reciprocal(rsums[:, i % 2], sums[:, i % 2]).then_inc(recip_done, 1)

            def px_rest(v, p, i):
                b, hf = divmod(i, 2)
                rest(flat(px[:, p, 1, b, 8 * hf:8 * hf + 8]), px_bank[:], flat(px[:, p, 0, b, 8 * hf:8 * hf + 8]),
                     px_hi, v + 1, px_lo)

            def probs_rest(v, i):
                rest(probs_t[:, i % 2, 1], tr_bank[:], probs_t[:, i % 2, 0], tr_hi, v + 1, tr_lo)

            def residual(n, p, nh):
                dve.wait_ge(yt_done, n + 1)
                dve.wait_ge(in_resid[p], nh * 16 + 16)
                dve.scalar_tensor_tensor(flat(x1[:, p]), r_bank[:, 0:GT], tanhs[:, 0:1], flat(x1[:, p]),
                                         ALU.mult, ALU.add).then_inc(x1_done, 1)
                dve.wait_ge(x1_done, n + 1)
                for c in range(TC):
                    dve.bn_stats(t_stats[:, c], x1[:, p, c]).then_inc(t_stats_step, 1)
                dve.wait_ge(t_stats_step, n * 2 * TC + TC)
                apart(dve)
                for c in range(TC):
                    dve.bn_aggr(t_moments[:, c], t_stats[:, c]).then_inc(t_stats_step, 1)

            def token_norm(n, p):
                dve.wait_ge(t_rstd_step, n * 2 + 2)
                dve.wait_ge(xn_free, n + 1)
                for c in range(TC):
                    dve.tensor_scalar(xn[:, p, c, 0:D], x1[:, p, c], t_moments[:, c, 0:1], t_rstd[:, c:c + 1],
                                      ALU.subtract, ALU.mult).then_inc(xn_done, 1)

            ROUTE = 6

            def route(n):
                done = [0]

                def step(*several):
                    for ins in several:
                        ins.then_inc(route_step, 1)
                        done[0] += 1
                    dve.wait_ge(route_step, n * ROUTE + done[0])

                dve.wait_ge(logits_done, n + 1)
                step(dve.tensor_copy(flat(logits[:]), r_bank[:, 0:TC * E]))
                apart(dve)
                step(*(dve.max(top[:, c], logits[:, c]) for c in range(TC)))
                dve.tensor_tensor(gap[:], top[:, :, 1], top[:, :, 0], ALU.subtract).then_inc(gap_done, 1)
                step(*(dve.max_index(top_i[:, c], top[:, c], logits[:, c]) for c in range(TC)))
                step(dve.tensor_copy(choice[:].rearrange("p (c k) -> p c k", k=TOP_K), top_i[:, :, 0:TOP_K]))
                dve.wait_ge(counts_step, n * TC + 1)
                dve.tensor_tensor(onehot[:], iota_e[:].unsqueeze(1).broadcast_to((P, TC * TOP_K, E)),
                                  choice[:].unsqueeze(2).broadcast_to((P, TC * TOP_K, E)), ALU.is_equal
                                  ).then_inc(onehot_done, 1)
                assert done[0] == ROUTE

            PLACE = 9

            def place(n, p):
                done = [0]

                def step(*several):
                    for ins in several:
                        ins.then_inc(place_step, 1)
                        done[0] += 1
                    dve.wait_ge(place_step, n * PLACE + done[0])

                dve.wait_ge(ratio_done, n + 1)
                dve.wait_ge(pos_done, n + 1)
                step(dve.tensor_tensor(placed[:], r_bank[:, 64:64 + TC * TOP_K * E].rearrange(
                         "p (c e) -> p c e", e=E), onehot[:], ALU.mult),
                     dve.tensor_scalar(ratio1[:], ratio[:], 1.0, None, ALU.add),
                     dve.scalar_tensor_tensor(base[:], choice[:], float(ROWS), k_offset[:], ALU.mult, ALU.add))
                step(dve.tensor_reduce(pos[:], placed[:], AX_X, ALU.add),
                     dve.reciprocal(wts[:, :, 0], ratio1[:]))
                step(dve.tensor_tensor(base_k[:], base[:], pos[:], ALU.add),
                     dve.tensor_scalar(valid[:], pos[:], float(CAP), None, ALU.is_lt),
                     dve.tensor_tensor(wts[:, :, 1], ratio[:], wts[:, :, 0], ALU.mult))
                step(dve.scalar_tensor_tensor(moved[:], base_k[:], float(-SLOTS), valid[:], ALU.add, ALU.mult))
                dve.tensor_scalar(slot[:, p], moved[:], float(SLOTS), None, ALU.add).then_inc(slot_done, 1)
                dve.wait_ge(wts_kept, n + 1)
                dve.tensor_scalar(wts_g[:], wts[:], tanhs[:, 1:2], None, ALU.mult).then_inc(wts_done, 1)
                assert done[0] == PLACE

            dve.wait_ge(tanh_done, 1)
            dve.wait_ge(consts, 1)
            def group(g, h, p, y, tail, ln, more):
                start = isinstance(g, int) and g == 0
                for i in range(HALVES):
                    u = g * HALVES + i
                    row_recip(u, i)
                    if ln and i == 7:
                        xt_rest(g + 2, p, r_bank)
                    if not (start and i < 2):
                        px_rest(u - 2, p if i >= 2 else 1 - p, (i - 2) % HALVES)
                    if not (start and i < 1):
                        probs_rest(u - 1, i - 1)
                    if not (not more and i == 7):
                        row_max(u + 1, i + 1, start and i < 1)
                    if tail and i == 1:
                        token_norm(g - 2, p)
                    if more:
                        q_rest(g + 1, 1 - p, i)
                    if start and i < 4:
                        ab_rest(4 + i)
                    if tail and i == 0:
                        residual(g - 2, p, h - 1)
                    if not more and i == 6:
                        residual(g - 1, 1 - p, NG // 2 - 1)
                    if not more and i == 7:
                        token_norm(g - 1, 1 - p)
                    if ln and i == 2:
                        ln_stats(g + 2, p, h + 2)
                    if more and i == 3:
                        group_mask(g + 1, 1 - p)
                    if tail and i == 3:
                        route(g - 2)
                    if ln and i == 4:
                        ln_normalise(g + 2, p)
                    if tail and i == 5:
                        place(g - 2, p)

            row_max(0, 0, True)

            schedule(dve, group)

            def turn_rest(e, p, j):
                dst, hi = turned_into(1, p, j), turned_into(0, p, j)
                rest(dst, turn_bank(e, j)[:, 0:dst.shape[1]], hi, turned_hi, e * TURNS + j + 1, turned_lo)

            px_rest(LAST - 2, 1, HALVES - 2)
            probs_rest(LAST - 1, 1)
            px_rest(LAST - 1, 1, HALVES - 1)
            route(NG - 2)
            place(NG - 2, 0)
            residual(NG - 1, 1, NG // 2 - 1)
            turn_rest(0, 0, 0)
            token_norm(NG - 1, 1)
            turn_rest(0, 0, 1)
            route(NG - 1)
            place(NG - 1, 1)
            turn_rest(0, 0, 2)
            turn_rest(0, 0, 3)
            turn_rest(0, 0, 4)

            def hidden_rest(e, f):
                rest(hid[:, 1, 1, f], hid_full[:, f], hid[:, 1, 0, f], hid_hi, e * UNITS + FC + f + 1, hid_lo[1])

            def copy_rows(e, p, piece):
                dve.wait_ge(ye_done, e * 2 + piece + 1)
                dst = flat(ye[:, p, slice(*BACK[piece])])
                dve.tensor_copy(dst, r_bank[:, 0:dst.shape[1]]).then_inc(ye_copied, 1)

            def expert(e, p, number):
                first = isinstance(e, int) and e == 0
                for u in range(UNITS):
                    dve.wait_ge(silu_done, e * UNITS + u + 1)
                    if u >= FC:
                        dve.wait_ge(hid_lo[0], e * FC + u - FC + 1)
                    dve.tensor_tensor(hid_full[:, u % 4], silu[:, u % 2], q_bank[u % 2][:, 0:CAP], ALU.mult
                                      ).then_inc(hid_done, 1)
                    if u == 0 and not first:
                        hidden_rest(e - 1, FC - 1)
                    if u > FC:
                        hidden_rest(e, u - FC - 1)
                    if u == 0 and not first and not (isinstance(e, int) and e == 1):
                        dve.wait_ge(ye_free, e - 1)
                    if u in (0, 4) and not first:
                        copy_rows(e - 1, 1 - p, u // 4)
                    if number is not None and u in TURN_AFTER:
                        turn_rest(e + 1, 1 - p, TURN_AFTER[u])
                if not first:
                    dve.wait_ge(ye_free, e)
                dve.tensor_tensor(row_i[:, p], xe[:, p, :, D], row_offset[:], ALU.add).then_inc(rows_done, 1)

            experts(dve, expert)
            hidden_rest(E - 1, FC - 1)
            dve.wait_ge(ye_free, E - 1)
            copy_rows(E - 1, 1, 0)
            copy_rows(E - 1, 1, 1)

            dve.wait_ge(in_x1, 16)
            dve.wait_ge(wts_kept, NG + 1)
            for r in range(4):
                dve.wait_ge(picked[r], 16 * TOP_K)
                for c in range(4 * r, 4 * r + 4):
                    dve.scalar_tensor_tensor(part[:, c], y_pick[:, 0, c], wts_all[:, c, 0:1], x1_all[:, c],
                                             ALU.mult, ALU.add).then_inc(first_part_done, 1)
            dve.wait_ge(first_part_done, NT)
            dve.wait_ge(second_part_done, NT)
            quarter = slice(NT - 4, NT)
            dve.tensor_tensor(final[:, quarter], part[:, quarter], scaled[:, quarter], ALU.add
                              ).then_inc(last_quarter_done, 1)


_INS = ['x', 'ctx_1024', 'mask_BxS2_bk0', 'g_xattn', 'g_ffn', 'L0_xattn_g1', 'L0_xattn_b1', 'L0_xattn_g2',
        'L0_xattn_b2', 'L0_xattn_Wq', 'L0_xattn_Wkv', 'L0_xattn_Wout', 'L0_ffn_gate_w', 'L0_ffn_wi_gate',
        'L0_ffn_wi_up', 'L0_ffn_wo']
_OUT = ((32, 64, 128), 'float32')


def kernel(**inputs):
    import numpy as _np
    import concourse.bacc as _bacc
    from concourse import mybir as _mybir
    from concourse.bass_utils import run_bass_kernel_spmd as _run

    nc = _bacc.Bacc("TRN2", target_bir_lowering=False, num_devices=1)
    arrays, args = {}, []
    for name in _INS:
        a = _np.ascontiguousarray(inputs[name])
        arrays[f"in_{name}_dram"] = a
        args.append(nc.dram_tensor(f"in_{name}_dram", a.shape, _mybir.dt.from_np(a.dtype), kind="ExternalInput").ap())
    out = nc.dram_tensor("out_0_dram", _OUT[0], _mybir.dt.from_np(_np.dtype(_OUT[1])), kind="ExternalOutput").ap()
    flamingo_block(nc, *args, out)
    r = _run(nc, [arrays], core_ids=[0])
    return r.results[0]["out_0_dram"]
```
